# Optimizing a Trainium2 kernel written in Bass

```python
import numpy as np
import jax
import jax.numpy as jnp

def _softmax(x, axis=-1):
    return jax.nn.softmax(x, axis=axis)

def _gelu(x):
    return jax.nn.gelu(x, approximate=True)

def _silu(x):
    return jax.nn.silu(x)

def _sigmoid(x):
    return jax.nn.sigmoid(x)

def _layernorm(x, axis=-1, eps=1e-05):
    m = jnp.mean(x, axis=axis, keepdims=True)
    v = jnp.var(x, axis=axis, keepdims=True)
    return (x - m) / jnp.sqrt(v + eps)

def _scatter_add(tgt, idx, src, axis=0):
    return tgt.at[idx].add(src)

def _segment_sum(src, seg, n):
    return jax.ops.segment_sum(src, seg, n)
kernel_name = 'mk_xattn_ffn_d1_seqx_r8_b7a7e5'

def setup_inputs(seed: int=0):
    np.random.seed(seed)
    _w = jnp.asarray

    def _rec_inputs():
        import jax
        import jax.numpy as jnp
        _rk = jax.random.key(seed)
        x = 2.818e-05 + 1 * jax.random.normal(jax.random.fold_in(_rk, 1), (4, 256, 256), jnp.float32)
        _lenS = 256 - jax.random.randint(jax.random.fold_in(_rk, 7), (4,), 0, max(1, 256 // 4) + 1, jnp.int32)
        _lenS2 = 256 - jax.random.randint(jax.random.fold_in(_rk, 8), (4,), 0, max(1, 256 // 4) + 1, jnp.int32)
        _ctx_1024P = jax.random.normal(jax.random.fold_in(_rk, 11), (4, 16, 128), jnp.float32)
        _ctx_1024c = jax.random.dirichlet(jax.random.fold_in(_rk, 511), 0.3 * jnp.ones((16,), jnp.float32), (4, 256))
        _ctx_1024t = jnp.einsum('bsk,bkd->bsd', _ctx_1024c, _ctx_1024P)
        _ctx_1024t = _ctx_1024t * jax.lax.rsqrt(jnp.mean(jnp.square(_ctx_1024t)) + 1e-12) * 0.953939
        ctx_1024 = 7.22013e-05 + 1.00017 * (_ctx_1024t + 0.3 * jax.random.normal(jax.random.fold_in(_rk, 611), (4, 256, 128), jnp.float32))
        return (x, ctx_1024)
    x, ctx_1024 = _rec_inputs()

    def _L0_xattn_setup():
        import jax, jax.numpy as jnp
        import numpy as np
        B_, L_, D_MODEL = (4, 256, 128)
        D_STATE, D_CONV, EXPAND = (16, 4, 2)
        D_INNER = EXPAND * D_MODEL
        DT_RANK = (D_MODEL + 15) // 16

        def silu(x):
            return x * jax.nn.sigmoid(x)
        key = jax.random.key(seed)
        ks = jax.random.split(key, 10)
        f32 = jnp.float32
        hidden_states = jax.random.normal(ks[0], (B_, L_, D_MODEL), dtype=f32)
        z = jax.random.normal(ks[1], (B_, D_INNER, L_), dtype=f32)
        in_proj_w = jax.random.normal(ks[2], (D_INNER, D_MODEL), dtype=f32) * 0.02
        conv_w = jax.random.normal(ks[3], (D_INNER, 1, D_CONV), dtype=f32) * 0.1
        conv_b = jax.random.normal(ks[4], (D_INNER,), dtype=f32) * 0.02
        x_proj_w = jax.random.normal(ks[5], (DT_RANK + 2 * D_STATE, D_INNER), dtype=f32) * 0.02
        dt_proj_w = jax.random.uniform(ks[6], (D_INNER, DT_RANK), dtype=f32, minval=-DT_RANK ** (-0.5), maxval=DT_RANK ** (-0.5))
        dt = jnp.exp(jax.random.uniform(ks[7], (D_INNER,), dtype=f32, minval=np.log(0.001), maxval=np.log(0.1)))
        dt_proj_b = jnp.log(jnp.expm1(dt))
        A_log = jnp.log(jnp.broadcast_to(jnp.arange(1, D_STATE + 1, dtype=f32), (D_INNER, D_STATE)))
        D = jnp.ones((D_INNER,), f32)
        return {'hidden_states': hidden_states, 'z': z, 'in_proj_w': in_proj_w, 'conv_w': conv_w, 'conv_b': conv_b, 'x_proj_w': x_proj_w, 'dt_proj_w': dt_proj_w, 'dt_proj_b': dt_proj_b, 'A_log': A_log, 'D': D}
    _L0_xattn_all = _L0_xattn_setup()
    _L0_xattn_in = {k: v for k, v in _L0_xattn_all.items() if k in ('in_proj_w', 'conv_w', 'conv_b', 'x_proj_w', 'dt_proj_w', 'dt_proj_b', 'A_log', 'D')}
    del _L0_xattn_all

    def _L0_ffn_setup():
        import jax, jax.numpy as jnp
        import numpy as np
        EPS = 1e-05

        def rms_norm(x):
            return x * jax.lax.rsqrt(jnp.mean(x * x, axis=-1, keepdims=True) + EPS)

        def act_quant(x):
            scale = 127.0 / jnp.clip(jnp.max(jnp.abs(x), axis=-1, keepdims=True), 1e-05)
            q = jnp.clip(jnp.round(x * scale), -128.0, 127.0) / scale
            return x + jax.lax.stop_gradient(q - x)

        def weight_quant(w):
            scale = 1.0 / jnp.clip(jnp.mean(jnp.abs(w)), 1e-05)
            q = jnp.clip(jnp.round(w * scale), -1.0, 1.0) / scale
            return w + jax.lax.stop_gradient(q - w)

        def bitlinear158(x, w, b):
            xq = act_quant(rms_norm(x))
            wq = weight_quant(w)
            return jnp.einsum('bsd,od->bso', xq, wq) + b

        def layer_norm(x, g, b):
            mu = jnp.mean(x, axis=-1, keepdims=True)
            var = jnp.mean((x - mu) ** 2, axis=-1, keepdims=True)
            return (x - mu) * jax.lax.rsqrt(var + EPS) * g + b
        key = jax.random.key(seed)
        ks = jax.random.split(key, 3)
        d, inner = (256, 1024)
        x = jax.random.normal(ks[0], (4, 256, d), dtype=jnp.float32)
        w1 = jax.random.normal(ks[1], (inner, d), dtype=jnp.float32) * 0.02
        b1 = jnp.zeros((inner,), jnp.float32)
        ln_g = jnp.ones((inner,), jnp.float32)
        ln_b = jnp.zeros((inner,), jnp.float32)
        w2 = jax.random.normal(ks[2], (d, inner), dtype=jnp.float32) * 0.02
        b2 = jnp.zeros((d,), jnp.float32)
        return {'x': x, 'w1': w1, 'b1': b1, 'ln_g': ln_g, 'ln_b': ln_b, 'w2': w2, 'b2': b2}
    _L0_ffn_all = _L0_ffn_setup()
    _L0_ffn_in = {k: v for k, v in _L0_ffn_all.items() if k in ('w1', 'b1', 'ln_g', 'ln_b', 'w2', 'b2')}
    del _L0_ffn_all
    return {'x': x, 'ctx_1024': ctx_1024, 'L0_xattn_in_proj_w': _L0_xattn_in['in_proj_w'], 'L0_xattn_conv_w': _L0_xattn_in['conv_w'], 'L0_xattn_conv_b': _L0_xattn_in['conv_b'], 'L0_xattn_x_proj_w': _L0_xattn_in['x_proj_w'], 'L0_xattn_dt_proj_w': _L0_xattn_in['dt_proj_w'], 'L0_xattn_dt_proj_b': _L0_xattn_in['dt_proj_b'], 'L0_xattn_A_log': _L0_xattn_in['A_log'], 'L0_xattn_D': _L0_xattn_in['D'], 'L0_ffn_w1': _L0_ffn_in['w1'], 'L0_ffn_b1': _L0_ffn_in['b1'], 'L0_ffn_ln_g': _L0_ffn_in['ln_g'], 'L0_ffn_ln_b': _L0_ffn_in['ln_b'], 'L0_ffn_w2': _L0_ffn_in['w2'], 'L0_ffn_b2': _L0_ffn_in['b2']}

def reference(x, ctx_1024, L0_xattn_in_proj_w, L0_xattn_conv_w, L0_xattn_conv_b, L0_xattn_x_proj_w, L0_xattn_dt_proj_w, L0_xattn_dt_proj_b, L0_xattn_A_log, L0_xattn_D, L0_ffn_w1, L0_ffn_b1, L0_ffn_ln_g, L0_ffn_ln_b, L0_ffn_w2, L0_ffn_b2):
    import jax
    import jax.numpy as jnp

    def _L0_xattn_ref(hidden_states, z, in_proj_w, conv_w, conv_b, x_proj_w, dt_proj_w, dt_proj_b, A_log, D):
        import jax, jax.numpy as jnp
        import numpy as np
        B_, L_, D_MODEL = (4, 256, 128)
        D_STATE, D_CONV, EXPAND = (16, 4, 2)
        D_INNER = EXPAND * D_MODEL
        DT_RANK = (D_MODEL + 15) // 16

        def silu(x):
            return x * jax.nn.sigmoid(x)
        Bsz, L, _ = hidden_states.shape
        d_inner, _, d_conv = conv_w.shape
        dt_rank = dt_proj_w.shape[1]
        d_state = A_log.shape[1]
        x = jnp.einsum('bld,ed->bel', hidden_states, in_proj_w)
        xc = jax.lax.conv_general_dilated(x, conv_w, window_strides=(1,), padding=[(d_conv - 1, 0)], feature_group_count=d_inner, dimension_numbers=('NCH', 'OIH', 'NCH'))
        x = silu(xc + conv_b[None, :, None])
        x_dbl = jnp.einsum('bdl,ed->bel', x, x_proj_w)
        dt_low, Bm, Cm = jnp.split(x_dbl, [dt_rank, dt_rank + d_state], axis=1)
        dt = jnp.einsum('brl,dr->bdl', dt_low, dt_proj_w)
        dt = jax.nn.softplus(dt + dt_proj_b[None, :, None])
        A = -jnp.exp(A_log)
        dt_t = jnp.moveaxis(dt, -1, 0)
        B_t = jnp.moveaxis(Bm, -1, 0)
        C_t = jnp.moveaxis(Cm, -1, 0)
        u_t = jnp.moveaxis(x, -1, 0)

        def step(state, inp):
            d, b, c, u = inp
            dA = jnp.exp(d[..., None] * A)
            state = state * dA + (d * u)[..., None] * b[:, None, :]
            y = jnp.einsum('bdn,bn->bd', state, c)
            return (state, y)
        state0 = jnp.zeros((Bsz, d_inner, d_state), x.dtype)
        _, ys = jax.lax.scan(step, state0, (dt_t, B_t, C_t, u_t))
        y = jnp.moveaxis(ys, 0, 2)
        y = y + D[None, :, None] * x
        y = y * silu(z)
        return jnp.swapaxes(y, 1, 2)

    def _L0_ffn_ref(x, w1, b1, ln_g, ln_b, w2, b2):
        import jax, jax.numpy as jnp
        import numpy as np
        EPS = 1e-05

        def rms_norm(x):
            return x * jax.lax.rsqrt(jnp.mean(x * x, axis=-1, keepdims=True) + EPS)

        def act_quant(x):
            scale = 127.0 / jnp.clip(jnp.max(jnp.abs(x), axis=-1, keepdims=True), 1e-05)
            q = jnp.clip(jnp.round(x * scale), -128.0, 127.0) / scale
            return x + jax.lax.stop_gradient(q - x)

        def weight_quant(w):
            scale = 1.0 / jnp.clip(jnp.mean(jnp.abs(w)), 1e-05)
            q = jnp.clip(jnp.round(w * scale), -1.0, 1.0) / scale
            return w + jax.lax.stop_gradient(q - w)

        def bitlinear158(x, w, b):
            xq = act_quant(rms_norm(x))
            wq = weight_quant(w)
            return jnp.einsum('bsd,od->bso', xq, wq) + b

        def layer_norm(x, g, b):
            mu = jnp.mean(x, axis=-1, keepdims=True)
            var = jnp.mean((x - mu) ** 2, axis=-1, keepdims=True)
            return (x - mu) * jax.lax.rsqrt(var + EPS) * g + b
        h = jax.nn.silu(bitlinear158(x, w1, b1))
        h = jax.nn.gelu(h, approximate=False)
        h = layer_norm(h, ln_g, ln_b)
        return bitlinear158(h, w2, b2)
    x = x + _L0_xattn_ref(ctx_1024, _layernorm(x, axis=-1), L0_xattn_in_proj_w, L0_xattn_conv_w, L0_xattn_conv_b, L0_xattn_x_proj_w, L0_xattn_dt_proj_w, L0_xattn_dt_proj_b, L0_xattn_A_log, L0_xattn_D)
    x = x + _L0_ffn_ref(_layernorm(x, axis=-1), L0_ffn_w1, L0_ffn_b1, L0_ffn_ln_g, L0_ffn_ln_b, L0_ffn_w2, L0_ffn_b2)
    return x

_drawn_inputs = setup_inputs


def setup_inputs(seed=0):
    import zlib

    import numpy as np

    out = dict(_drawn_inputs(seed))
    spreads = {'L0_xattn_D': (1.0, 0.6),
     'L0_ffn_b1': (0.0, 2.0),
     'L0_ffn_ln_g': (1.0, 0.6),
     'L0_ffn_ln_b': (0.0, 2.0),
     'L0_ffn_b2': (0.0, 2.0)}
    factors = {'ctx_1024': 3.434,
     'L0_xattn_in_proj_w': 3.443,
     'L0_xattn_conv_w': 3.546,
     'L0_xattn_conv_b': 5.672,
     'L0_xattn_x_proj_w': 8.0,
     'L0_xattn_dt_proj_w': 8.0,
     'L0_xattn_dt_proj_b': 8.0,
     'L0_xattn_A_log': 8.0,
     'L0_ffn_w1': 8.0,
     'L0_ffn_w2': 7.887}
    for name, (base, spread) in spreads.items():
        noise = np.random.default_rng([zlib.crc32(name.encode()), seed]).standard_normal(out[name].shape)
        drawn = base * np.exp(spread * noise) if base else spread * noise
        out[name] = jnp.asarray(drawn.astype(out[name].dtype))
    for name, factor in factors.items():
        out[name] = (out[name] * factor).astype(out[name].dtype)
    return out
```

```python
from contextlib import ExitStack

import concourse.bass as bass
from concourse import mybir

F32 = mybir.dt.float32
BF16 = mybir.dt.bfloat16
I32 = mybir.dt.int32
ACT = mybir.ActivationFunctionType
ALU = mybir.AluOpType
AX = mybir.AxisListType

P = 128
NB, L, D = 4, 256, 256
DM = 128
NS, R, TAPS = 16, 8, 4
HID = 1024
HALVES = D // P
PAIRS = NB // 2
PW = 2 * L
GRP = NS // 2
UNITS = PAIRS * HALVES * GRP
UW = 2 * PW
RING = 4
TILES = NB * L // P
TPP = TILES // PAIRS
KB = HID // P
EPS = 1e-5
ROUND = 12582912.0
SMALL_E = 2.0 ** -8
C_CONV, C_CB, C_DTB, C_D, C_A = 0, TAPS, TAPS + 1, TAPS + 2, TAPS + 3
CH = C_A + NS
XM = 3 * 2 * NS + R


def mixer_ffn(nc, x, ctxT, inwT, xprojT, dtpT, chan, w1T, w2T, rows, ident, out):
    with ExitStack() as ctx:
        def sb(name, shape, dt=F32):
            return ctx.enter_context(nc.sbuf_tensor(name, shape, dt))

        def sem(name):
            return ctx.enter_context(nc.semaphore(name))

        x_nat = sb("x_nat", [P, HALVES, NB, D])
        siluz = sb("siluz", [P, HALVES, NB, L])
        ctx_sb = sb("ctx_sb", [P, NB * L])
        inw_sb = sb("inw_sb", [P, D])
        xproj_sb = sb("xproj_sb", [P, HALVES, XM])
        dtp_sb = sb("dtp_sb", [XM, D])
        chan_sb = sb("chan_sb", [P, HALVES, CH])
        id_f = sb("id_f", [P, P])
        id_b = sb("id_b", [P, P], BF16)
        sel = sb("sel", [3 * 2 * NS, 2 * NS], BF16)
        ones = sb("ones", [P, P])
        conv = sb("conv", [P, HALVES, NB * L])
        u = sb("u", [P, HALVES, NB * L])
        dt = sb("dt", [P, HALVES, NB * L])
        dtu = sb("dtu", [P, HALVES, NB * L])
        negA = sb("negA", [P, HALVES, NS])
        bc_parts = sb("bc_parts", [3 * 2 * NS, PAIRS, PW], BF16)
        bc_rest = sb("bc_rest", [3 * 2 * NS, PW])
        bc_mid = sb("bc_mid", [3 * 2 * NS, PW], BF16)
        dt_low = sb("dt_low", [XM, PAIRS, PW])
        c_bc = sb("c_bc", [P, NS, PW])
        dA = sb("dA", [P, RING, UW])
        dBu = sb("dBu", [P, 2, UW])
        st = sb("st", [P, RING, UW])
        yg = sb("yg", [P, PW])
        w1q = sb("w1q", [P, HALVES, HID], BF16)
        w2q = sb("w2q", [P, KB, D], BF16)
        rows_sb = sb("rows_sb", [P, 3 * HID + D])
        w_raw = sb("w_raw", [P, 4096])
        hid = w_raw[:, 0:2 * HID].rearrange("p (r n) -> p r n", r=2)
        val = w_raw[:, 2 * HID:4 * HID].rearrange("p (r n) -> p r n", r=2)
        x1 = sb("x1", [P, TPP, D])
        xc = sb("xc", [P, TPP, D])
        x1b = sb("x1b", [P, PAIRS, TPP, D])
        q1 = sb("q1", [P, TPP, D], BF16)
        q1T = sb("q1T", [P, TPP, HALVES, P], BF16)
        q2 = sb("q2", [P, 2, HID], BF16)
        q2T = sb("q2T", [P, 2, KB, P], BF16)
        res = sb("res", [P, 2, D])
        stats = sb("stats", [P, 16, 6])
        zmv = sb("zmv", [P, HALVES * NB, 2])
        zr = sb("zr", [P, 4, HALVES * NB])
        mv1 = sb("mv1", [P, TPP, 2])
        sm1 = sb("sm1", [P, 12, TPP])
        mv2 = sb("mv2", [P, 2, 2])
        sm2 = sb("sm2", [P, 2, 16])
        os1 = sb("os1", [P, TILES])
        os2 = sb("os2", [P, TILES])
        wabs = sb("wabs", [P, 2])
        wmean = sb("wmean", [P, 2, 2])
        am2 = sb("am2", [P, 2])
        m_half = sb("m_half", [P, 8])
        m_one = sb("m_one", [P, 8])
        sp_abs = dA[:, 0, 0:PW * 2].rearrange("p (r n) -> p r n", r=2)
        sp_e = st[:, 0, :].rearrange("p (r n) -> p r n", r=2)
        sp_ln = st[:, 1, :].rearrange("p (r n) -> p r n", r=2)
        sp_relu = st[:, 2, :].rearrange("p (r n) -> p r n", r=2)
        sp_mask = st[:, 3, :].rearrange("p (r n) -> p r n", r=2)
        sp_ser = dBu[:, 1, :].rearrange("p (r n) -> p r n", r=2)

        ps = ctx.enter_context(nc.psum_tensor("ps", [P, 8 * 512], F32))

        def bank(n, k=1):
            return ps[:, n * 512:(n + k) * 512]

        yacc = bank(0)
        bps = bank(1, 2)
        yT = bank(3)
        mm1 = bank(4, 2)
        tq = bank(6).bitcast(BF16)
        mm2 = ps[:, 7 * 512:7 * 512 + D]

        in_ctx, in_inw, in_chan, in_x, in_proj, in_dtp, in_id = (
            sem("in_" + n) for n in ("ctx", "inw", "chan", "x", "proj", "dtp", "id"))
        in_w1, in_w2, in_rows = sem("in_w1"), sem("in_w2"), sem("in_rows")
        out_done = [sem("out_done_even"), sem("out_done_odd")]
        consts_set = sem("consts_set")
        ids_cast = sem("ids_cast")
        xin_ready = sem("xin_ready")
        tap_done = sem("tap_done")
        taps_done = sem("taps_done")
        z_stats = sem("z_stats")
        z_aggr = sem("z_aggr")
        z_small = sem("z_small")
        u_ready = sem("u_ready")
        z_ready = sem("z_ready")
        xdbl_ready = sem("xdbl_ready")
        dtlow_ready = sem("dtlow_ready")
        split_step = sem("split_step")
        dtraw_ready = sem("dtraw_ready")
        sp_act = sem("sp_act")
        expA_done = sem("expA_done")
        negA_ready = sem("negA_ready")
        sp_pool = sem("sp_pool")
        dt_step = sem("dt_step")
        wabs_done = sem("wabs_done")
        wsum_ready = sem("wsum_ready")
        wmean_step = sem("wmean_step")
        wq_step = sem("wq_step")
        c_staged = sem("c_staged")
        c_copied = sem("c_copied")
        b_spread = sem("b_spread")
        dbu_done = sem("dbu_done")
        exp_done = sem("exp_done")
        scanned = sem("scanned")
        prod_done = sem("prod_done")
        summed = sem("summed")
        gate_step = sem("gate_step")
        y_turned = sem("y_turned")
        x1_half = sem("x1_half")
        bn1_done = sem("bn1_done")
        mv1_done = sem("mv1_done")
        xc_done = sem("xc_done")
        amax1_done = sem("amax1_done")
        x1b_done = sem("x1b_done")
        sm1_step = sem("sm1_step")
        q1_scaled = sem("q1_scaled")
        q1_done = sem("q1_done")
        q1_turned = sem("q1_turned")
        q1T_done = sem("q1T_done")
        mm1_done = sem("mm1_done")
        pre_done = sem("pre_done")
        silu_done, gelu_done, norm_done, sq_done, w_done, q2T_done = (
            sem(n) for n in ("silu_done", "gelu_done", "norm_done", "sq_done", "w_done", "q2T_done"))
        bn2_done, mv2_done, gained, valued, amax2_done = (
            sem(n) for n in ("bn2_done", "mv2_done", "gained", "valued", "amax2_done"))
        sm2a_step = sem("sm2a_step")
        sm2b_step = sem("sm2b_step")
        q2_done = sem("q2_done")
        q2_turned, mm2_done, res_done = sem("q2_turned"), sem("mm2_done"), sem("res_done")

        def cols(t, h, p):
            return t[:, h, p * PW:(p + 1) * PW]

        def by_batch(ap):
            return ap.rearrange("p (b l) -> p b l", b=2)

        GS = [(p, h) for p in range(PAIRS) for h in range(HALVES)]
        block = ctx.enter_context(nc.Block())

        T = UNITS
        vec_at, act_at, pool_at, pe_at = ({} for _ in range(4))

        def put(table, pos, *work):
            table.setdefault(pos, []).append(work)

        for g in range(PAIRS * HALVES):
            end = GRP * (g + 1)
            put(vec_at, end + 1, "gate", g)
            put(pe_at, end + 2, "turn_y", g)
            put(vec_at, end + 2, "x1", g)
        for p in range(PAIRS):
            a = GRP * HALVES * (p + 1) + 3
            put(vec_at, a, "ln1", p)
            put(pool_at, a, "small1", p)
            put(vec_at, a + 1, "quant1", p)
            put(pe_at, a + 2, "turn_q1", p)
            put(act_at, a + 2, "copy_q1", p)
        for g, base in enumerate((21, 27, 38, 43)):
            for i in range(2):
                t = 2 * g + i
                b = base + i
                put(pe_at, b, "mm1", t)
                put(vec_at, b, "pre", t)
                put(act_at, b + 1, "silu", t)
                put(act_at, base + 2, "gelu", t)
                put(vec_at, b + 3, "bn2", t)
                put(pool_at, b + 3, "small2a", t)
                put(act_at, b + 4, "norm", t)
                put(vec_at, b + 4, "affine", t)
                put(act_at, b + 5, "square", t)
                put(pool_at, b + 5, "small2b", t)
                put(act_at, b + 6, "scale2", t)
                put(pool_at, b + 6, "quant2", t)
                put(pe_at, b + 7, "turn_q2", t)
                put(act_at, b + 7, "copy_q2", t)
                put(pe_at, b + 8, "mm2", t)
                put(vec_at, b + 8, "res", t)
        END = 60

        @block.sync
        def _(sp):
            sp.dma_start(ctx_sb[:, :], ctxT).then_inc(in_ctx, 16)
            sp.dma_start(chan_sb[:, :, :], chan).then_inc(in_chan, 16)
            for h in range(HALVES):
                sp.dma_start(x_nat[:, h], x[:, h * P:(h + 1) * P, :].rearrange("b p d -> p b d")).then_inc(in_x, 16)
            sp.dma_start(w_raw[:, 0:2048].rearrange("p (k n) -> p k n", k=HALVES),
                         w1T.rearrange("(k p) n -> p k n", p=P)).then_inc(in_w1, 16)
            sp.dma_start(w_raw[:, 2048:4096].rearrange("p (k n) -> p k n", k=KB),
                         w2T.rearrange("(k p) n -> p k n", p=P)).then_inc(in_w2, 16)
            sp.dma_start(rows_sb[:, :], rows.partition_broadcast(P)).then_inc(in_rows, 16)
            for t in range(TILES):
                b, lt = t // 2, t % 2
                sp.wait_ge(res_done, t + 1)
                sp.dma_start(out[b, lt * P:(lt + 1) * P, :], res[:, t % 2, :]).then_inc(out_done[t % 2], 16)
            for s in out_done:
                sp.wait_ge(s, 16 * TILES // 2)

        @block.tensor
        def _(pe):
            pe.wait_ge(in_ctx, 16)
            pe.wait_ge(in_inw, 16)
            for g, (p, h) in enumerate(GS):
                nc.tensor.matmul(bank(4 + g), inw_sb[:, h * P:(h + 1) * P], ctx_sb[:, p * PW:(p + 1) * PW],
                                 start=True, stop=True).then_inc(xin_ready, 1)
            pe.wait_ge(in_proj, 16)
            for p in range(PAIRS):
                pe.wait_ge(u_ready, 2 * p + 2)
                o = bank(3 if p == 0 else 0)[0:XM, :]
                for h in range(HALVES):
                    mm = nc.tensor.matmul(o, xproj_sb[:, h, :], cols(u, h, p), start=h == 0, stop=h == 1)
                mm.then_inc(xdbl_ready, 1)
            pe.wait_ge(in_dtp, 16)
            pe.wait_ge(taps_done, 3 * len(GS))
            for g, (p, h) in enumerate(GS):
                pe.wait_ge(dtlow_ready, p + 1)
                nc.tensor.matmul(bank(4 + g), dtp_sb[96:XM, h * P:(h + 1) * P], dt_low[96:XM, p, :],
                                 start=True, stop=True).then_inc(dtraw_ready, 1)
            pe.wait_ge(wabs_done, 2)
            pe.wait_ge(consts_set, 1)
            nc.tensor.matmul(bank(2)[:, 0:2], ones[:, :], wabs[:, :], start=True, stop=True).then_inc(wsum_ready, 1)

            def spread(o, p, row):
                return nc.tensor.matmul(o, sel[:, row:row + 1].to_broadcast([3 * 2 * NS, P]), bc_parts[:, p, :],
                                        start=True, stop=True)

            def stage_c(c):
                p, ng = c // GRP, c % GRP
                if c < 2:
                    pe.wait_ge(sp_act, 4 * len(GS))
                if c >= 2:
                    pe.wait_ge(c_copied, c - 1)
                for i in range(2):
                    mm = spread(bank(4 + 2 * (c % 2) + i), p, NS + 2 * ng + i)
                mm.then_inc(c_staged, 1)

            def spread_b(k):
                p, ng = k // (2 * GRP), k % GRP
                if k == 0:
                    pe.wait_ge(wmean_step, 2)
                else:
                    pe.wait_ge(dbu_done, k)
                for i in range(2):
                    mm = spread(bank(1 + i), p, 2 * ng + i)
                mm.then_inc(b_spread, 1)

            def sum_states(k):
                g, ng = k // GRP, k % GRP
                if ng == 0 and g:
                    pe.wait_ge(gate_step, 2 * g - 1)
                pe.wait_ge(prod_done, k + 1)
                for i in range(2):
                    mm = nc.tensor.matmul(yacc, id_f[:, :], st[:, k % RING, i * PW:(i + 1) * PW],
                                          start=ng == 0 and i == 0, stop=ng == GRP - 1 and i == 1)
                mm.then_inc(summed, 1)

            def turn_y(g):
                pe.wait_ge(gate_step, 2 * g + 2)
                if g:
                    pe.wait_ge(x1_half, g)
                for i in range(TPP):
                    mm = nc.tensor.transpose(yT[:, i * P:(i + 1) * P], yg[:, i * P:(i + 1) * P], id_f[:, :])
                mm.then_inc(y_turned, 1)

            def turn_q1(p):
                pe.wait_ge(q1_done, p + 1)
                if p == 0:
                    pe.wait_ge(c_copied, 2 * GRP)
                else:
                    pe.wait_ge(q2T_done, TPP)
                for t in range(TPP):
                    for h in range(HALVES):
                        o = (t * HALVES + h) * P
                        mm = nc.tensor.transpose(tq[:, o:o + P], q1[:, t, h * P:(h + 1) * P], id_b[:, :])
                mm.then_inc(q1_turned, 1)

            def do_mm1(t):
                pe.wait_ge(q1T_done, t // TPP + 1)
                pe.wait_ge(wq_step, 6)
                if t:
                    pe.wait_ge(pre_done, t)
                for n in range(2):
                    for k in range(HALVES):
                        mm = nc.tensor.matmul(mm1[:, n * 512:(n + 1) * 512], q1T[:, t % TPP, k, :],
                                              w1q[:, k, n * 512:(n + 1) * 512], start=k == 0, stop=k == 1)
                mm.then_inc(mm1_done, 1)

            def turn_q2(t):
                pe.wait_ge(q2_done, t + 1)
                pe.wait_ge(q1T_done, t // TPP + 1)
                if t:
                    pe.wait_ge(q2T_done, t)
                for k in range(KB):
                    mm = nc.tensor.transpose(tq[:, k * P:(k + 1) * P], q2[:, t % 2, k * P:(k + 1) * P], id_b[:, :])
                mm.then_inc(q2_turned, 1)

            def do_mm2(t):
                pe.wait_ge(q2T_done, t + 1)
                if t:
                    pe.wait_ge(res_done, t)
                for k in range(KB):
                    mm = nc.tensor.matmul(mm2, q2T[:, t % 2, k, :], w2q[:, k, :], start=k == 0, stop=k == KB - 1)
                mm.then_inc(mm2_done, 1)

            work = {"turn_y": turn_y, "turn_q1": turn_q1, "mm1": do_mm1, "turn_q2": turn_q2, "mm2": do_mm2}
            pe.wait_ge(ids_cast, 4)
            pe.wait_ge(split_step, 6)
            spread_b(0)
            stage_c(0)
            pe.wait_ge(in_id, 16)
            for k in range(END):
                if k + 1 < UNITS:
                    spread_b(k + 1)
                if k + 1 < GRP:
                    stage_c(k + 1)
                if GRP <= k - 3 < 2 * GRP:
                    stage_c(k - 3)
                if 0 <= k - 1 < UNITS:
                    sum_states(k - 1)
                for name, i in pe_at.get(k, []):
                    work[name](i)

        @block.scalar
        def _(act):
            act.dma_start(inw_sb[:, :], inwT).then_inc(in_inw, 16)
            act.dma_start(xproj_sb[:, :, :], xprojT).then_inc(in_proj, 16)
            act.dma_start(dtp_sb[96:XM, :], dtpT).then_inc(in_dtp, 16)
            act.dma_start(id_f[:, :], ident).then_inc(in_id, 16)
            act.wait_ge(in_chan, 16)
            for g, (p, h) in enumerate(GS):
                act.wait_ge(xin_ready, g + 1)
                nc.scalar.activation(cols(conv, h, p), bank(4 + g), ACT.Identity,
                                     bias=chan_sb[:, h, C_CB:C_CB + 1],
                                     scale=chan_sb[:, h, C_CONV + 3:C_CONV + 4]).then_inc(tap_done, 1)
            for g, (p, h) in enumerate(GS):
                act.wait_ge(taps_done, 3 * g + 3)
                nc.scalar.activation(cols(u, h, p), cols(conv, h, p), ACT.Silu).then_inc(u_ready, 1)
                if g == 1:
                    act.wait_ge(z_small, 4)
                    for h2 in range(HALVES):
                        for b in range(NB):
                            j = h2 * NB + b
                            nc.scalar.activation(siluz[:, h2, b, :], x_nat[:, h2, b, :], ACT.Silu,
                                                 bias=zr[:, 3, j:j + 1], scale=zr[:, 1, j:j + 1]).then_inc(z_ready, 1)
            nc.scalar.preload_act_table_set("natural_log_exp_and_others")
            nc.scalar.activation(negA[:, :, :], chan_sb[:, :, C_A:CH], ACT.Exp).then_inc(expA_done, 1)
            for p in range(PAIRS):
                act.wait_ge(xdbl_ready, p + 1)
                o = bank(3 if p == 0 else 0)
                nc.scalar.activation(dt_low[96:XM, p, :], o[96:XM, :], ACT.Copy).then_inc(dtlow_ready, 1)
            for g, (p, h) in enumerate(GS):
                r = g % 2
                b = chan_sb[:, h, C_DTB:C_DTB + 1]
                act.wait_ge(dtraw_ready, g + 1)
                if g >= 2:
                    act.wait_ge(dt_step, 3 * (g - 2) + 3)
                    act.wait_ge(sp_pool, 3 * (g - 2) + 3)
                nc.scalar.activation(sp_abs[:, r], bank(4 + g), ACT.Abs, bias=b).then_inc(sp_act, 1)
                nc.scalar.activation(sp_relu[:, r], bank(4 + g), ACT.Relu, bias=b).then_inc(sp_act, 1)
                act.wait_ge(sp_act, 4 * g + 1)
                nc.scalar.activation(sp_e[:, r], sp_abs[:, r], ACT.Exp, scale=-1.0).then_inc(sp_act, 1)
                act.wait_ge(sp_act, 4 * g + 3)
                nc.scalar.activation(sp_ln[:, r], sp_e[:, r], ACT.Ln, bias=1.0).then_inc(sp_act, 1)
            for i, s in enumerate((in_w1, in_w2)):
                act.wait_ge(s, 16)
                act.wait_ge(dt_step, 3 * len(GS)) if i == 0 else None
                nc.scalar.activation(c_bc[:, 4 * i:4 * i + 4, :], w_raw[:, 2048 * i:2048 * (i + 1)].rearrange(
                    "p (n c) -> p n c", c=PW), ACT.Abs, accum_out=wabs[:, i:i + 1]).then_inc(wabs_done, 1)

            def exps(k):
                p, h, ng = k // (2 * GRP), k // GRP % 2, k % GRP
                if k == 0:
                    act.wait_ge(negA_ready, 1)
                    act.wait_ge(consts_set, 2)
                if k >= RING:
                    act.wait_ge(scanned, k - RING + 1)
                for i in range(2):
                    n = 2 * ng + i
                    o = dA[:, k % RING, i * PW:(i + 1) * PW]
                    e = nc.scalar.activation(by_batch(o)[:, :, 1:L], by_batch(cols(dt, h, p))[:, :, 1:L], ACT.Exp,
                                             scale=negA[:, h, n:n + 1])
                e.then_inc(exp_done, 1)

            def copy_c(c):
                ng = c % GRP
                act.wait_ge(c_staged, c + 1)
                if c == 0:
                    act.wait_ge(wabs_done, 2)
                if c >= GRP:
                    act.wait_ge(prod_done, c + 1)
                nc.scalar.activation(c_bc[:, 2 * ng:2 * ng + 2, :].rearrange("p a b -> p (a b)"),
                                     bank(4 + 2 * (c % 2), 2), ACT.Copy).then_inc(c_copied, 1)

            def copy_q1(p):
                act.wait_ge(q1_turned, p + 1)
                if p:
                    act.wait_ge(mm1_done, TPP)
                nc.scalar.activation(q1T[:, :, :, :].rearrange("p t h n -> p (t h n)"), tq, ACT.Copy).then_inc(q1T_done, 1)

            def silu(t):
                act.wait_ge(pre_done, t + 1)
                nc.scalar.activation(hid[:, t % 2], hid[:, t % 2], ACT.Silu).then_inc(silu_done, 1)

            def gelu(t):
                act.wait_ge(silu_done, t + 1)
                nc.scalar.activation(hid[:, t % 2], hid[:, t % 2], ACT.Gelu).then_inc(gelu_done, 1)

            def norm(t):
                act.wait_ge(sm2a_step, 3 * t + 3)
                nc.scalar.activation(hid[:, t % 2], hid[:, t % 2], ACT.Identity, bias=sm2[:, t % 2, 3:4],
                                     scale=sm2[:, t % 2, 1:2]).then_inc(norm_done, 1)

            def square(t):
                act.wait_ge(valued, t + 1)
                nc.scalar.activation(hid[:, t % 2], val[:, t % 2], ACT.Square,
                                     accum_out=sm2[:, t % 2, 4:5]).then_inc(sq_done, 1)

            def scale2(t):
                act.wait_ge(sm2b_step, 7 * t + 7)
                act.wait_ge(amax2_done, t + 1)
                nc.scalar.activation(val[:, t % 2], val[:, t % 2], ACT.Identity, bias=ROUND,
                                     scale=sm2[:, t % 2, 11:12]).then_inc(w_done, 1)

            def copy_q2(t):
                act.wait_ge(q2_turned, t + 1)
                if t >= 2:
                    act.wait_ge(mm2_done, t - 1)
                nc.scalar.activation(q2T[:, t % 2].rearrange("p k n -> p (k n)"), tq, ACT.Copy).then_inc(q2T_done, 1)

            work = {"copy_q1": copy_q1, "silu": silu, "gelu": gelu, "norm": norm, "square": square,
                    "scale2": scale2, "copy_q2": copy_q2}
            exps(0)
            copy_c(0)
            exps(1)
            exps(2)
            for k in range(END):
                if k + 3 < UNITS:
                    exps(k + 3)
                if k + 1 < GRP:
                    copy_c(k + 1)
                if GRP <= k - 3 < 2 * GRP:
                    copy_c(k - 3)
                for name, i in act_at.get(k, []):
                    work[name](i)

        @block.gpsimd
        def _(pool):
            nc.gpsimd.memset(ones[:, :], 1.0)
            nc.gpsimd.memset(m_half[:, :], -0.5)
            nc.gpsimd.memset(m_one[:, :], -1.0).then_inc(consts_set, 1)
            pool.wait_ge(z_aggr, HALVES * NB)
            pool.wait_ge(consts_set, 1)
            nc.gpsimd.tensor_scalar(zr[:, 0, :], zmv[:, :, 1], EPS, None, ALU.add).then_inc(z_small, 1)
            pool.wait_ge(z_small, 1)
            nc.gpsimd.tensor_tensor(zr[:, 1, :], zr[:, 0, :], m_half[:, :], ALU.pow).then_inc(z_small, 1)
            pool.wait_ge(z_small, 2)
            nc.gpsimd.tensor_tensor(zr[:, 2, :], zr[:, 1, :], zmv[:, :, 0], ALU.mult).then_inc(z_small, 1)
            pool.wait_ge(z_small, 3)
            nc.gpsimd.tensor_scalar(zr[:, 3, :], zr[:, 2, :], -1.0, None, ALU.mult).then_inc(z_small, 1)
            pool.wait_ge(expA_done, 1)
            nc.gpsimd.tensor_scalar(negA[:, :, :], negA[:, :, :], -1.0, None, ALU.mult).then_inc(negA_ready, 1)
            for g in range(len(GS)):
                r = g % 2
                pool.wait_ge(sp_act, 4 * g + 3)
                if g >= 2:
                    pool.wait_ge(dt_step, 3 * (g - 2) + 3)
                nc.gpsimd.tensor_scalar(sp_ser[:, r], sp_e[:, r], -0.5, 1.0, ALU.mult, ALU.add).then_inc(sp_pool, 1)
                nc.gpsimd.tensor_scalar(sp_mask[:, r], sp_e[:, r], SMALL_E, None, ALU.is_lt).then_inc(sp_pool, 1)
                pool.wait_ge(sp_pool, 3 * g + 1)
                nc.gpsimd.tensor_tensor(sp_ser[:, r], sp_ser[:, r], sp_e[:, r], ALU.mult).then_inc(sp_pool, 1)
            pool.wait_ge(sp_act, 4 * len(GS))
            nc.gpsimd.memset(dA[:, :, :].rearrange("p r (s l) -> p (r s) l", l=L)[:, :, 0:1], 0.0).then_inc(consts_set, 1)
            for i in range(2):
                w = w_raw[:, 2048 * i:2048 * (i + 1)]
                q = (w1q if i == 0 else w2q)[:, :, :].rearrange("p k n -> p (k n)")
                pool.wait_ge(wmean_step, 3)
                pool.wait_ge(wabs_done, 2)
                nc.gpsimd.tensor_scalar(w, w, wmean[:, i, 1:2], -1.0,
                                        ALU.mult, ALU.max).then_inc(wq_step, 1)
                pool.wait_ge(wq_step, 3 * i + 1)
                nc.gpsimd.tensor_scalar(w, w, 1.0, ROUND, ALU.min, ALU.add).then_inc(wq_step, 1)
                pool.wait_ge(wq_step, 3 * i + 2)
                nc.gpsimd.tensor_scalar(q, w, ROUND, None, ALU.subtract).then_inc(wq_step, 1)

            def prod(k):
                ng = k % GRP
                pool.wait_ge(c_copied, k // (2 * GRP) * GRP + ng + 1)
                pool.wait_ge(scanned, k + 1)
                s = st[:, k % RING, :]
                nc.gpsimd.tensor_tensor(s, s, c_bc[:, 2 * ng:2 * ng + 2, :].rearrange("p a b -> p (a b)"),
                                        ALU.mult).then_inc(prod_done, 1)

            def small1(p):
                base = [13 * p]

                def step(ins):
                    base[0] += 1
                    ins.then_inc(sm1_step, 1)
                    pool.wait_ge(sm1_step, base[0])

                s = [sm1[:, i, :] for i in range(12)]
                half, one = m_half[:, 0:TPP], m_one[:, 0:TPP]
                ts, tt = nc.gpsimd.tensor_scalar, nc.gpsimd.tensor_tensor
                pool.wait_ge(mv1_done, TPP * (p + 1))
                if p:
                    pool.wait_ge(q1_scaled, TPP * p)
                step(ts(s[0], mv1[:, :, 1], EPS, None, ALU.add))
                step(tt(s[1], s[0], half, ALU.pow))
                step(tt(s[2], mv1[:, :, 1], s[1], ALU.mult))
                step(tt(s[3], s[2], s[1], ALU.mult))
                step(ts(s[4], s[3], EPS, None, ALU.add))
                step(tt(s[5], s[4], half, ALU.pow))
                step(tt(s[6], s[5], s[1], ALU.mult))
                pool.wait_ge(amax1_done, p + 1)
                step(tt(s[7], s[6], sm1[:, 11, :], ALU.mult))
                step(ts(s[8], s[7], EPS, 1.0 / 127.0, ALU.max, ALU.mult))
                step(tt(s[9], s[8], one, ALU.pow))
                step(tt(s[10], s[9], s[6], ALU.mult))
                pool.wait_ge(wmean_step, 3)
                step(ts(os1[:, TPP * p:TPP * (p + 1)], s[8], wmean[:, 0, 0:1], None, ALU.mult))
                pool.wait_ge(x1_half, 2 * p + 2)
                pool.wait_ge(in_rows, 16)
                nc.gpsimd.tensor_tensor(x1b[:, p], x1[:, :, :],
                                        rows_sb[:, 3 * HID:3 * HID + D].unsqueeze(1).to_broadcast([P, TPP, D]),
                                        ALU.add).then_inc(x1b_done, 1)
                pool.wait_ge(x1b_done, p + 1)
                pool.sem_inc(sm1_step, 1)

            def stepper(done, n):
                base = [n]

                def step(ins):
                    base[0] += 1
                    ins.then_inc(done, 1)
                    pool.wait_ge(done, base[0])
                return step

            def small2a(t):
                step, s = stepper(sm2a_step, 3 * t), sm2[:, t % 2, :]
                pool.wait_ge(mv2_done, t + 1)
                if t >= 2:
                    pool.wait_ge(w_done, t - 1)
                step(nc.gpsimd.tensor_scalar(s[:, 0:1], mv2[:, t % 2, 1:2], EPS, None, ALU.add))
                step(nc.gpsimd.tensor_tensor(s[:, 1:2], s[:, 0:1], m_half[:, 0:1], ALU.pow))
                step(nc.gpsimd.tensor_scalar(s[:, 3:4], mv2[:, t % 2, 0:1], s[:, 1:2], -1.0, ALU.mult, ALU.mult))

            def small2b(t):
                step, s = stepper(sm2b_step, 7 * t), sm2[:, t % 2, :]
                pool.wait_ge(sq_done, t + 1)
                step(nc.gpsimd.tensor_scalar(s[:, 5:6], s[:, 4:5], 1.0 / HID, EPS, ALU.mult, ALU.add))
                step(nc.gpsimd.tensor_tensor(s[:, 6:7], s[:, 5:6], m_half[:, 0:1], ALU.pow))
                pool.wait_ge(amax2_done, t + 1)
                step(nc.gpsimd.tensor_scalar(s[:, 7:8], am2[:, t % 2:t % 2 + 1], s[:, 6:7], EPS, ALU.mult, ALU.max))
                step(nc.gpsimd.tensor_scalar(s[:, 8:9], s[:, 7:8], 1.0 / 127.0, None, ALU.mult))
                step(nc.gpsimd.tensor_tensor(s[:, 9:10], s[:, 8:9], m_one[:, 0:1], ALU.pow))
                step(nc.gpsimd.tensor_tensor(s[:, 11:12], s[:, 9:10], s[:, 6:7], ALU.mult))
                step(nc.gpsimd.tensor_tensor(os2[:, t:t + 1], s[:, 8:9], wmean[:, 1, 0:1], ALU.mult))

            def quant2(t):
                pool.wait_ge(w_done, t + 1)
                if t >= 2:
                    pool.wait_ge(q2_turned, t - 1)
                nc.gpsimd.tensor_scalar(q2[:, t % 2, :], val[:, t % 2], ROUND, None, ALU.subtract).then_inc(q2_done, 1)

            work = {"small1": small1, "small2a": small2a, "small2b": small2b, "quant2": quant2}
            for k in range(END):
                if k < UNITS:
                    prod(k)
                for name, i in pool_at.get(k, []):
                    work[name](i)

        @block.vector
        def _(dve):
            dve.wait_ge(in_chan, 16)
            for g, (p, h) in enumerate(GS):
                dve.wait_ge(tap_done, g + 1)
                src, dst = by_batch(bank(4 + g)), by_batch(cols(conv, h, p))
                for s in range(1, TAPS):
                    j = C_CONV + TAPS - 1 - s
                    if s > 1:
                        dve.wait_ge(taps_done, 3 * g + s - 1)
                    nc.vector.scalar_tensor_tensor(out=dst[:, :, s:L], in0=src[:, :, 0:L - s],
                                                   scalar=chan_sb[:, h, j:j + 1], in1=dst[:, :, s:L],
                                                   op0=ALU.mult, op1=ALU.add).then_inc(taps_done, 1)
                if g == 1:
                    dve.wait_ge(in_x, 16 * HALVES)
                    for j in range(HALVES * NB):
                        nc.vector.bn_stats(stats[:, j, :], x_nat[:, j // NB, j % NB, :]).then_inc(z_stats, 1)
                    for j in range(HALVES * NB):
                        dve.wait_ge(z_stats, j + 1)
                        nc.vector.bn_aggr(zmv[:, j, :], stats[:, j, :]).then_inc(z_aggr, 1)
                    dve.wait_ge(in_id, 16)
                    for j in range(3):
                        nc.vector.tensor_copy(sel[32 * j:32 * j + 32, :],
                                                  id_f[32 * j:32 * j + 32, 32 * j:32 * j + 32]).then_inc(ids_cast, 1)
                    nc.vector.tensor_copy(id_b[:, :], id_f[:, :]).then_inc(ids_cast, 1)
            for p in range(PAIRS):
                n = 5 * p
                v = bank(3 if p == 0 else 0)[0:96, :]
                parts = bc_parts[:, p, :]
                dve.wait_ge(xdbl_ready, p + 1)
                nc.vector.tensor_copy(parts, v).then_inc(split_step, 1)
                dve.wait_ge(split_step, n + 1)
                nc.vector.tensor_tensor(bc_rest[:, :], v, parts, ALU.subtract).then_inc(split_step, 1)
                dve.wait_ge(split_step, n + 2)
                nc.vector.tensor_copy(parts[32:64, :], bc_rest[32:64, :]).then_inc(split_step, 1)
                nc.vector.tensor_copy(bc_mid[64:96, :], bc_rest[64:96, :]).then_inc(split_step, 1)
                dve.wait_ge(split_step, n + 4)
                nc.vector.tensor_tensor(parts[64:96, :], bc_rest[64:96, :], bc_mid[64:96, :],
                                        ALU.subtract).then_inc(split_step, 1)
                dve.wait_ge(split_step, n + 5)
                for h in range(HALVES):
                    g = 2 * p + h
                    r = g % 2
                    dve.wait_ge(sp_act, 4 * g + 4)
                    dve.wait_ge(sp_pool, 3 * g + 3)
                    nc.vector.copy_predicated(sp_ln[:, r], sp_mask[:, r].bitcast(I32), sp_ser[:, r]).then_inc(dt_step, 1)
                    dve.wait_ge(dt_step, 3 * g + 1)
                    nc.vector.tensor_tensor(cols(dt, h, p), sp_ln[:, r], sp_relu[:, r], ALU.add).then_inc(dt_step, 1)
                    dve.wait_ge(dt_step, 3 * g + 2)
                    nc.vector.tensor_tensor(cols(dtu, h, p), cols(dt, h, p), cols(u, h, p), ALU.mult).then_inc(dt_step, 1)
            dve.wait_ge(wsum_ready, 1)
            for i in range(2):
                nc.vector.tensor_scalar(wmean[:, i, 0:1], bank(2)[:, i:i + 1], 1.0 / (HID * D), EPS, ALU.mult, ALU.max)\
                    .then_inc(wmean_step, 1)
            dve.wait_ge(wmean_step, 2)
            nc.vector.reciprocal(wmean[:, :, 1], wmean[:, :, 0]).then_inc(wmean_step, 1)

            def scan(k):
                p, h = k // (2 * GRP), k // GRP % 2
                dve.wait_ge(b_spread, k + 1)
                if k == 0:
                    dve.wait_ge(sp_pool, 3 * len(GS))
                if k >= 2:
                    dve.wait_ge(scanned, k - 1)
                nc.vector.tensor_tensor(dBu[:, k % 2, :].rearrange("p (n c) -> p n c", n=2),
                                        cols(dtu, h, p).unsqueeze(1).to_broadcast([P, 2, PW]),
                                        bps.rearrange("p (n c) -> p n c", n=2), ALU.mult).then_inc(dbu_done, 1)
                dve.wait_ge(dbu_done, k + 1)
                dve.wait_ge(exp_done, k + 1)
                if k >= RING:
                    dve.wait_ge(summed, k - RING + 1)
                nc.vector.tensor_tensor_scan(st[:, k % RING, :], dA[:, k % RING, :], dBu[:, k % 2, :], 0.0,
                                             ALU.mult, ALU.add).then_inc(scanned, 1)

            def gate(g):
                p, h = g // 2, g % 2
                dve.wait_ge(summed, GRP * (g + 1))
                if g:
                    dve.wait_ge(y_turned, g)
                nc.vector.scalar_tensor_tensor(out=yg[:, :], in0=cols(u, h, p), scalar=chan_sb[:, h, C_D:C_D + 1],
                                               in1=yacc, op0=ALU.mult, op1=ALU.add).then_inc(gate_step, 1)
                dve.wait_ge(gate_step, 2 * g + 1)
                dve.wait_ge(z_ready, HALVES * NB)
                nc.vector.tensor_tensor(yg[:, :], yg[:, :], siluz[:, h, 2 * p:2 * p + 2, :].rearrange(
                    "p b l -> p (b l)"), ALU.mult).then_inc(gate_step, 1)

            def add_x1(g):
                p, h = g // 2, g % 2
                dve.wait_ge(y_turned, g + 1)
                if g == 2:
                    dve.wait_ge(x1b_done, 1)
                    dve.wait_ge(xc_done, TPP)
                nc.vector.tensor_tensor(x1[:, :, h * P:(h + 1) * P].rearrange("p (b t) d -> p b t d", b=2),
                                        x_nat[:, :, 2 * p:2 * p + 2, h * P:(h + 1) * P].rearrange("p t b d -> p b t d"),
                                        yT.rearrange("p (b t d) -> p b t d", b=2, t=2), ALU.add).then_inc(x1_half, 1)

            def ln1(p):
                dve.wait_ge(x1_half, 2 * p + 2)
                if p == 0:
                    dve.wait_ge(z_aggr, HALVES * NB)
                for t in range(TPP):
                    nc.vector.bn_stats(stats[:, t, :], x1[:, t, :]).then_inc(bn1_done, 1)
                if p:
                    dve.wait_ge(sm1_step, 13 * p)
                for t in range(TPP):
                    dve.wait_ge(bn1_done, TPP * p + t + 1)
                    nc.vector.bn_aggr(mv1[:, t, :], stats[:, t, :]).then_inc(mv1_done, 1)
                for t in range(TPP):
                    dve.wait_ge(mv1_done, TPP * p + t + 1)
                    nc.vector.tensor_scalar(xc[:, t, :], x1[:, t, :], mv1[:, t, 0:1], None, ALU.subtract)\
                        .then_inc(xc_done, 1)
                dve.wait_ge(xc_done, TPP * (p + 1))
                nc.vector.tensor_reduce(sm1[:, 11, :], xc[:, :, :], AX.X, ALU.max,
                                        apply_absolute_value=True).then_inc(amax1_done, 1)

            def quant1(p):
                dve.wait_ge(sm1_step, 13 * p + 12)
                dve.wait_ge(amax1_done, p + 1)
                for t in range(TPP):
                    nc.vector.tensor_scalar(xc[:, t, :], xc[:, t, :], sm1[:, 10, t:t + 1], ROUND, ALU.mult, ALU.add)\
                        .then_inc(q1_scaled, 1)
                dve.wait_ge(q1_scaled, TPP * (p + 1))
                if p:
                    dve.wait_ge(q1_turned, p)
                nc.vector.tensor_scalar(q1[:, :, :], xc[:, :, :], ROUND, None, ALU.subtract).then_inc(q1_done, 1)

            def pre(t):
                dve.wait_ge(mm1_done, t + 1)
                dve.wait_ge(in_rows, 16)
                dve.wait_ge(wq_step, 6)
                if t >= 2:
                    dve.wait_ge(sq_done, t - 1)
                nc.vector.scalar_tensor_tensor(out=hid[:, t % 2], in0=mm1, scalar=os1[:, t:t + 1],
                                               in1=rows_sb[:, 0:HID], op0=ALU.mult, op1=ALU.add).then_inc(pre_done, 1)

            def bn2(t):
                dve.wait_ge(gelu_done, t + 1)
                for i in range(2):
                    nc.vector.bn_stats(stats[:, 8 + 2 * (t % 2) + i, :], hid[:, t % 2, 512 * i:512 * (i + 1)])\
                        .then_inc(bn2_done, 1)
                dve.wait_ge(bn2_done, 2 * t + 2)
                if t >= 2:
                    dve.wait_ge(norm_done, t - 1)
                nc.vector.bn_aggr(mv2[:, t % 2, :], stats[:, 8 + 2 * (t % 2):10 + 2 * (t % 2), :].rearrange(
                    "p a b -> p (a b)")).then_inc(mv2_done, 1)

            def affine(t):
                dve.wait_ge(norm_done, t + 1)
                if t >= 2:
                    dve.wait_ge(q2_done, t - 1)
                v = val[:, t % 2]
                nc.vector.tensor_tensor(v, hid[:, t % 2], rows_sb[:, HID:2 * HID], ALU.mult).then_inc(gained, 1)
                dve.wait_ge(gained, t + 1)
                nc.vector.tensor_tensor(v, v, rows_sb[:, 2 * HID:3 * HID], ALU.add).then_inc(valued, 1)
                dve.wait_ge(valued, t + 1)
                if t >= 2:
                    dve.wait_ge(sm2b_step, 7 * (t - 2) + 3)
                nc.vector.tensor_reduce(am2[:, t % 2:t % 2 + 1], v, AX.X, ALU.max,
                                        apply_absolute_value=True).then_inc(amax2_done, 1)

            def result(t):
                p = t // TPP
                dve.wait_ge(mm2_done, t + 1)
                dve.wait_ge(sm2b_step, 7 * t + 7)
                dve.wait_ge(x1b_done, p + 1)
                if t >= 2:
                    dve.wait_ge(out_done[t % 2], 16 * (t // 2))
                nc.vector.scalar_tensor_tensor(out=res[:, t % 2, :], in0=mm2, scalar=os2[:, t:t + 1],
                                               in1=x1b[:, p, t % TPP, :], op0=ALU.mult, op1=ALU.add).then_inc(res_done, 1)

            work = {"gate": gate, "x1": add_x1, "ln1": ln1, "quant1": quant1, "pre": pre, "bn2": bn2,
                    "affine": affine, "res": result}
            for k in range(END):
                if k < UNITS:
                    scan(k)
                for name, i in vec_at.get(k, []):
                    work[name](i)


def kernel(x, ctx_1024, L0_xattn_in_proj_w, L0_xattn_conv_w, L0_xattn_conv_b, L0_xattn_x_proj_w,
           L0_xattn_dt_proj_w, L0_xattn_dt_proj_b, L0_xattn_A_log, L0_xattn_D, L0_ffn_w1, L0_ffn_b1,
           L0_ffn_ln_g, L0_ffn_ln_b, L0_ffn_w2, L0_ffn_b2):
    import numpy as np
    import concourse.bacc as bacc
    from concourse.bass_utils import run_bass_kernel_spmd

    def halves(a):
        return np.ascontiguousarray(a.reshape(HALVES, P, -1).transpose(1, 0, 2))

    f = np.asarray
    xp = f(L0_xattn_x_proj_w)
    bc = xp[R:]
    chan = np.concatenate([f(L0_xattn_conv_w)[:, 0, :], f(L0_xattn_conv_b)[:, None], f(L0_xattn_dt_proj_b)[:, None],
                           f(L0_xattn_D)[:, None], f(L0_xattn_A_log)], axis=1)
    data = {
        "x": np.ascontiguousarray(f(x)),
        "ctxT": np.ascontiguousarray(f(ctx_1024).reshape(NB * L, DM).T),
        "inwT": np.ascontiguousarray(f(L0_xattn_in_proj_w).T),
        "xprojT": halves(np.concatenate([bc, bc, bc, xp[:R]], axis=0).T),
        "dtpT": np.ascontiguousarray(f(L0_xattn_dt_proj_w).T),
        "chan": halves(chan),
        "w1T": np.ascontiguousarray(f(L0_ffn_w1).T),
        "w2T": np.ascontiguousarray(f(L0_ffn_w2).T),
        "rows": np.concatenate([f(L0_ffn_b1), f(L0_ffn_ln_g), f(L0_ffn_ln_b), f(L0_ffn_b2)]),
        "ident": np.eye(P, dtype=np.float32),
    }
    nc = bacc.Bacc("TRN2", target_bir_lowering=False, num_devices=1)
    args = [nc.dram_tensor(n, a.shape, mybir.dt.from_np(a.dtype), kind="ExternalInput").ap() for n, a in data.items()]
    out = nc.dram_tensor("out", (NB, L, D), F32, kind="ExternalOutput").ap()
    mixer_ffn(nc, *args, out)
    r = run_bass_kernel_spmd(nc, [data], core_ids=[0])
    return r.results[0]["out"]
```

```python
from contextlib import ExitStack

import concourse.bass as bass
from concourse import mybir

F32 = mybir.dt.float32
BF16 = mybir.dt.bfloat16
I32 = mybir.dt.int32
ACT = mybir.ActivationFunctionType
ALU = mybir.AluOpType
AX = mybir.AxisListType

P = 128
NB, L, D = 4, 256, 256
DM = 128
NS, R, TAPS = 16, 8, 4
HID = 1024
HALVES = D // P
SG = 4
GROUPS = NS // SG
UPB = HALVES * GROUPS
UNITS = NB * UPB
UW = SG * L
DA_RING, DBU_RING, ST_RING = 6, 2, 6
AHEAD = 2
TPB = L // P
TILES = NB * TPB
KB = HID // P
HSLOTS = 4
EPS = 1e-5
LEVELS = 127.0
ROUND = 12582912.0
SMALL_E = 2.0 ** -8
C_CONV, C_CB, C_DTB, C_D, C_A = 0, TAPS, TAPS + 1, TAPS + 2, TAPS + 3
CH = C_A + NS
XM = 2 * NS + R


STEPS = ("ln1", "root1", "quant1", "turn_q1", "add_b2", "copy_q1", "mm1", "silu", "gelu", "bn2", "root2a", "norm",
         "gain", "shift", "amax2", "square", "root2b", "scales2", "scale2", "quant2", "turn_q2", "copy_q2", "mm2", "res")
LAGS = ((2, 2, 3, 4, 4, 3, 4, 6, 7, 9, 8, 8, 10, 10, 11, 11, 11, 12, 13, 13, 13, 14, 15, 16),
        (2, 2, 3, 4, 4, 3, 4, 6, 7, 9, 8, 8, 10, 10, 11, 11, 11, 12, 13, 13, 13, 14, 15, 16),
        (2, 2, 3, 4, 4, 4, 4, 5, 5, 6, 6, 7, 7, 7, 8, 8, 8, 9, 9, 10, 9, 10, 11, 12),
        (2, 2, 3, 3, 4, 3, 3, 4, 6, 6, 6, 7, 6, 7, 7, 7, 7, 9, 9, 10, 10, 10, 12, 12))
APARTS = ((0, 0, 0, 0, 0, 0, 0, 0, 0, 0, 0, 0, 1, 1, 1, 1, 1, 1, 1, 1, 1, 1, 1, 1),
          (0, 0, 0, 0, 0, 0, 0, 0, 0, 0, 0, 0, 1, 1, 1, 1, 1, 1, 1, 1, 1, 1, 1, 1),
          (0, 0, 0, 0, 0, 0, 0, 0, 0, 0, 0, 0, 1, 1, 1, 1, 1, 1, 1, 1, 1, 1, 1, 1),
          (0, 0, 0, 0, 0, 0, 0, 0, 0, 0, 0, 0, 1, 1, 1, 1, 1, 1, 1, 1, 1, 1, 1, 1))
GATE = (1, 1, 2)
DTLAGS = ({"xdbl": 0, "copy_xd": 0, "dtraw": 0, "dt_bias": 2, "dt_neg": 2, "dt_exp": 2, "dt_series": 2, "dt_mask": 4,
           "dt_sum": 4},
          {"xdbl": -1, "copy_xd": 0, "dtraw": 0, "dt_bias": 0, "dt_neg": 2, "dt_exp": 2, "dt_series": 2, "dt_mask": 3,
           "dt_sum": 5})
EARLY = {("convolve", 2): 0, ("convolve", 3): 2, ("silu_u", 1): 0, ("silu_u", 2): 4, ("silu_u", 3): 4,
         ("silu_z", 0): 4, ("silu_z", 1): 4, ("silu_z", 2): 15, ("silu_z", 3): 13, ("sum_weights", 0): 5,
         ("sum_weights", 1): 6, ("wsum", 0): 8, ("wmean", 0): 9, ("scale_weights", 0): 10, ("scale_weights", 1): 11,
         ("clip_weights", 0): 11, ("clip_weights", 1): 12}
VECTOR = ("wmean", "clip_weights", "dt_neg", "dt_mask", "dt_sum", "ln1", "quant1", "bn2", "gain", "amax2", "scales2", "res")
SCALAR = ("silu_u", "sum_weights", "silu_z", "scale_weights", "copy_xd", "dt_bias", "dt_exp", "copy_q1", "silu", "gelu", "norm", "square", "scale2", "copy_q2")
POOL = ("dt_series", "root1", "add_b2", "root2a", "shift", "root2b", "quant2")
PER_TILE = ("mm1", "silu", "gelu", "bn2", "root2a", "norm", "gain", "shift", "amax2", "square", "root2b", "scales2",
            "scale2", "quant2", "turn_q2", "copy_q2", "mm2", "res")


def schedule():
    vec, act, pool, pe = {}, {}, {}, {}

    def put(table, at, *work):
        table.setdefault(at, []).append(work)

    def place(step, at, i):
        last = step == "quant2" and i >= TILES - TPB
        table = vec if step in VECTOR or last else act if step in SCALAR else pool if step in POOL else pe
        put(table, at, step, i)

    for (step, i), at in EARLY.items():
        place(step, at, i)
    for b in range(1, NB):
        for step, lag in DTLAGS[min(b, 2) - 1].items():
            place(step, UPB * (b - 1) + lag, b)
    for b in range(NB):
        for h in range(HALVES):
            e = UPB * b + GROUPS * (h + 1)
            put(vec, e + GATE[0], "gate", 2 * b + h)
            put(pe, e + GATE[1], "turn_y", 2 * b + h)
            put(vec, e + GATE[2], "x1", 2 * b + h)
        e = UPB * (b + 1)
        for step, lag, apart in zip(STEPS, LAGS[b], APARTS[b]):
            if step in PER_TILE:
                for i in range(TPB):
                    place(step, e + lag + i * apart, TPB * b + i)
            else:
                place(step, e + lag, b)
    order = {"gate": -3, "turn_y": -2, "x1": -1}
    for table in (vec, pe):
        for works in table.values():
            works.sort(key=lambda w: order.get(w[0], 0))
    return vec, act, pool, pe, UNITS + max(LAGS[-1]) + 2


def mixer_ffn(nc, x, ctxT, inwT, xprojT, dtpT, chan, taps, w1T, w2T, rows, ident, spread, out):
    vec_at, act_at, pool_at, pe_at, END = schedule()
    with ExitStack() as ctx:
        def sb(name, shape, dt=F32):
            return ctx.enter_context(nc.sbuf_tensor(name, shape, dt))

        def sem(name):
            return ctx.enter_context(nc.semaphore(name))

        x_nat = sb("x_nat", [P, HALVES, NB, D])
        siluz = sb("siluz", [P, HALVES, NB, L])
        ctx_sb = sb("ctx_sb", [P, NB * L])
        inw_sb = sb("inw_sb", [P, D])
        taps_sb = sb("taps_sb", [P, TAPS, D])
        inw_taps = taps_sb
        xproj_sb = sb("xproj_sb", [P, HALVES, XM])
        dtp_sb = sb("dtp_sb", [XM, D])
        chan_sb = sb("chan_sb", [P, HALVES, CH])
        id_f = sb("id_f", [P, P])
        id_b = sb("id_b", [P, P], BF16)
        ones = sb("ones", [P, P])
        cv = sb("cv", [P, HALVES, NB, L])
        u = cv
        dt = sb("dt", [P, HALVES, 2, L])
        dtu = sb("dtu", [P, HALVES, 2, L])
        negA = sb("negA", [P, HALVES, NS])
        xd = sb("xd", [XM, NB, L])
        sp_v, sp_e, sp_ln, sp_mask, sp_ser = (sb(n, [P, HALVES, L]) for n in ("sp_v", "sp_e", "sp_ln", "sp_mask", "sp_ser"))
        bc = sb("bc", [P, GROUPS, 2, SG, L])
        dA = sb("dA", [P, DA_RING, UW])
        dBu = sb("dBu", [P, DBU_RING, UW])
        st = sb("st", [P, ST_RING, UW])
        yg = sb("yg", [P, 2, L])
        w1q = sb("w1q", [P, HALVES, HID], BF16)
        w2q = sb("w2q", [P, KB, D], BF16)
        rows_sb = sb("rows_sb", [P, 3 * HID + D])
        w_raw = sb("w_raw", [P, 2, 2048])
        hid = w_raw[:, :, :].rearrange("p a (b n) -> p (a b) n", b=2)
        xc = sb("xc", [P, TPB, D])
        q1 = sb("q1", [P, TPB, D], BF16)
        q1T = sb("q1T", [P, TPB, HALVES, P], BF16)
        diag = sb("diag", [P, 2, P])
        q2 = sb("q2", [P, 2, HID], BF16)
        q2T = sb("q2T", [P, 2, KB, P], BF16)
        junk = sb("junk", [P, HID], BF16)
        res = sb("res", [P, 2, D])
        stats = sb("stats", [P, 8 + 2 + 4, 6])
        zmv = sb("zmv", [P, HALVES * NB, 2])
        zr = sb("zr", [P, 4, HALVES * NB])
        mv1 = sb("mv1", [P, TPB, 2])
        amax1 = sb("amax1", [P, TPB])
        sm1 = sb("sm1", [P, 8, TPB])
        mv2 = sb("mv2", [P, 2, 2])
        am2 = sb("am2", [P, 2])
        sm2 = sb("sm2", [P, 2, 16])
        wabs = sb("wabs", [P, 2])
        wmean = sb("wmean", [P, 2, 2])
        m_half = sb("m_half", [P, 8])

        ps = ctx.enter_context(nc.psum_tensor("ps", [P, 8 * 512], F32))

        def bank(n, k=1):
            return ps[:, n * 512:(n + k) * 512]

        yacc = bank(0)[:, 0:L]
        head = bank(1)
        mm2, yT = bank(2)[:, 0:D], bank(2)[:, D:2 * D]
        tq = bank(3).bitcast(BF16)
        mm1 = [bank(4, 2), bank(6, 2)]
        xin = [bank(1), bank(7), bank(4), bank(5)]

        in_ctx0, in_ctx, in_inw, in_chan, in_taps, in_x, in_proj, in_dtp, in_id, in_w1, in_w2, in_rows = (
            sem("in_" + n) for n in ("ctx0", "ctx", "inw", "chan", "taps", "x", "proj", "dtp", "id", "w1", "w2", "rows"))
        spread_out = sem("spread_out")
        b_in, c_in = ([sem(f"{n}_in{g}") for g in range(GROUPS)] for n in "bc")
        out_done = [sem("out_done_even"), sem("out_done_odd")]
        consts_set, zeros_set, id_cast = sem("consts_set"), sem("zeros_set"), sem("id_cast")
        z_stats, z_aggr, z_small, z_ready = sem("z_stats"), sem("z_aggr"), sem("z_small"), sem("z_ready")
        expA_done, negA_ready = sem("expA_done"), sem("negA_ready")
        wabs_done, wsum_ready, wmean_step = sem("wabs_done"), sem("wsum_ready"), sem("wmean_step")
        w_scaled, w_clip = sem("w_scaled"), sem("w_clip")
        taps_scaled = sem("taps_scaled")
        xin_ready, conv_step, u_ready = sem("xin_ready"), sem("conv_step"), sem("u_ready")
        xdbl_ready, xd_copied, dtraw_ready = sem("xdbl_ready"), sem("xd_copied"), sem("dtraw_ready")
        dt_v, dt_negd, dt_e, dt_ln = sem("dt_v"), sem("dt_negd"), sem("dt_e"), sem("dt_ln")
        dt_ser, dt_step, dt_cp = sem("dt_ser"), sem("dt_step"), sem("dt_cp")
        dbu_done, exp_done, scanned, prod_done, summed = (
            sem(n) for n in ("dbu_done", "exp_done", "scanned", "prod_done", "summed"))
        gate_step, y_turned, x1_half = sem("gate_step"), sem("y_turned"), sem("x1_half")
        bn1_done, mv1_done, xc_done, amax1_done, root1_step, sc1_step = (
            sem(n) for n in ("bn1_done", "mv1_done", "xc_done", "amax1_done", "root1_step", "sc1_step"))
        q1_scaled, q1_done, q1_turned, q1T_done, b2_added = (
            sem(n) for n in ("q1_scaled", "q1_done", "q1_turned", "q1T_done", "b2_added"))
        diag_done, mm1_done, silu_done, gelu_done, bn2_done, mv2_done, root2a_step, norm_done, gained, shifted = (
            sem(n) for n in ("diag_done", "mm1_done", "silu_done", "gelu_done", "bn2_done", "mv2_done",
                             "root2a_step", "norm_done", "gained", "shifted"))
        amax2_done, sq_done, root2b_step, sc2_step, w_done, q2_done, q2_turned, q2T_done, mm2_done, res_done = (
            sem(n) for n in ("amax2_done", "sq_done", "root2b_step", "sc2_step", "w_done", "q2_done",
                             "q2_turned", "q2T_done", "mm2_done", "res_done"))

        def where(k):
            return k // UPB, k // GROUPS % HALVES, k % GROUPS

        block = ctx.enter_context(nc.Block())

        @block.sync
        def _(sp):
            sp.dma_start(ctx_sb[:, 0:L], ctxT[:, 0:L]).then_inc(in_ctx0, 16)
            sp.dma_start(chan_sb[:, :, :], chan).then_inc(in_chan, 16)
            sp.dma_start(ctx_sb[:, L:NB * L], ctxT[:, L:NB * L]).then_inc(in_ctx, 16)
            for h in range(HALVES):
                sp.dma_start(x_nat[:, h], x[:, h * P:(h + 1) * P, :].rearrange("b p d -> p b d")).then_inc(in_x, 16)

            def store(t):
                sp.wait_ge(res_done, t + 1)
                sp.dma_start(out[t // TPB, t % TPB * P:(t % TPB + 1) * P, :], res[:, t % 2, :])\
                    .then_inc(out_done[t % 2], 16)

            for b in range(NB):
                sp.wait_ge(xd_copied, b + 1)
                sp.dma_start(spread[b], xd[0:2 * NS, b, :]).then_inc(spread_out, 16)
                sp.wait_ge(spread_out, 16 * (b + 1))

                def load(g, c):
                    if b:
                        sp.wait_ge((dbu_done, prod_done)[c], UPB * b - GROUPS + g + 1)
                    r = SG * (2 * g + c)
                    sp.dma_start(bc[:, g, c].rearrange("p s l -> p (s l)"),
                                 spread[b, r:r + SG, :].rearrange("s l -> (s l)").partition_broadcast(P))\
                        .then_inc((b_in, c_in)[c][g], 16)

                load(0, 0)
                for g in range(GROUPS):
                    if g + 1 < GROUPS:
                        load(g + 1, 0)
                    load(g, 1)
                if b == 0:
                    sp.dma_start(w_raw[:, 0].rearrange("p (k n) -> p k n", k=HALVES),
                                 w1T.rearrange("(k p) n -> p k n", p=P)).then_inc(in_w1, 16)
                    sp.dma_start(w_raw[:, 1].rearrange("p (k n) -> p k n", k=KB),
                                 w2T.rearrange("(k p) n -> p k n", p=P)).then_inc(in_w2, 16)
                    sp.dma_start(rows_sb[:, :], rows.partition_broadcast(P)).then_inc(in_rows, 16)
            for t in range(TILES):
                store(t)
            for s in out_done:
                sp.wait_ge(s, 16 * TILES // 2)

        @block.tensor
        def _(pe):
            turned, made = [0], [0]

            pe.wait_ge(in_inw, 16)
            pe.wait_ge(in_ctx0, 16)
            for h in range(HALVES):
                mm = nc.tensor.matmul(xin[0][:, h * L:(h + 1) * L], inw_sb[:, h * P:(h + 1) * P], ctx_sb[:, 0:L],
                                      start=True, stop=True)
            mm.then_inc(xin_ready, 1)

            def convolve(b):
                pe.wait_ge(in_ctx, 16)
                pe.wait_ge(taps_scaled, 1)
                for h in range(HALVES):
                    for s in range(TAPS):
                        mm = nc.tensor.matmul(xin[b][:, h * L + s:(h + 1) * L], inw_taps[:, s, h * P:(h + 1) * P],
                                              ctx_sb[:, b * L:(b + 1) * L - s], start=s == 0, stop=s == TAPS - 1)
                mm.then_inc(xin_ready, 1)

            def xdbl(b):
                if b == 0:
                    pe.wait_ge(in_proj, 16)
                else:
                    pe.wait_ge(dt_v, HALVES * b)
                pe.wait_ge(u_ready, b + 1)
                for h in range(HALVES):
                    mm = nc.tensor.matmul(head[0:XM, 0:L], xproj_sb[:, h, :], u[:, h, b, :], start=h == 0, stop=h == 1)
                mm.then_inc(xdbl_ready, 1)

            def dtraw(b):
                if b == 0:
                    pe.wait_ge(in_dtp, 16)
                pe.wait_ge(xd_copied, b + 1)
                for h in range(HALVES):
                    mm = nc.tensor.matmul(head[:, h * L:(h + 1) * L], dtp_sb[2 * NS:XM, h * P:(h + 1) * P],
                                          xd[2 * NS:XM, b, :], start=True, stop=True)
                mm.then_inc(dtraw_ready, 1)

            def sum_states(k):
                b, h, ng = where(k)
                if ng == 0 and k:
                    pe.wait_ge(gate_step, 2 * (k // GROUPS) - 1)
                pe.wait_ge(prod_done, k + 1)
                for i in range(SG):
                    mm = nc.tensor.matmul(yacc, id_f[:, :], st[:, k % ST_RING, i * L:(i + 1) * L],
                                          start=ng == 0 and i == 0, stop=ng == GROUPS - 1 and i == SG - 1)
                mm.then_inc(summed, 1)

            def wsum(_):
                pe.wait_ge(wabs_done, 2)
                pe.wait_ge(consts_set, 1)
                nc.tensor.matmul(bank(6)[:, 0:2], ones[:, :], wabs[:, :], start=True, stop=True).then_inc(wsum_ready, 1)

            def turn_y(g):
                pe.wait_ge(gate_step, 2 * g + 2)
                if g:
                    pe.wait_ge(x1_half, g)
                if made[0]:
                    pe.wait_ge(res_done, made[0])
                for i in range(TPB):
                    mm = nc.tensor.transpose(yT[:, i * P:(i + 1) * P], yg[:, g % 2, i * P:(i + 1) * P], id_f[:, :])
                mm.then_inc(y_turned, 1)
                turned[0] = g + 1

            def turn_q1(b):
                pe.wait_ge(q1_done, b + 1)
                if b == 0:
                    pe.wait_ge(id_cast, 1)
                else:
                    pe.wait_ge(q2T_done, made_q2[0])
                for t in range(TPB):
                    for h in range(HALVES):
                        o = (t * HALVES + h) * P
                        mm = nc.tensor.transpose(tq[:, o:o + P], q1[:, t, h * P:(h + 1) * P], id_b[:, :])
                mm.then_inc(q1_turned, 1)
                made_q1[0] = b + 1

            def do_mm1(t):
                b, i = t // TPB, t % TPB
                pe.wait_ge(diag_done, t + 1)
                if t == 0:
                    pe.wait_ge(in_rows, 16)
                    pe.wait_ge(w_clip, 4)
                    pe.wait_ge(u_ready, NB)
                if b:
                    pe.wait_ge(silu_done, t - 1)
                cols = [slice(n * 512, (n + 1) * 512) for n in range(2)]
                for c in cols:
                    nc.tensor.matmul(mm1[i][:, c], diag[:, i, :], rows_sb[:, c], start=True, stop=False)
                pe.wait_ge(q1T_done, b + 1)
                for c in cols:
                    for k in range(HALVES):
                        mm = nc.tensor.matmul(mm1[i][:, c], q1T[:, i, k, :], w1q[:, k, c], start=False, stop=k == 1)
                mm.then_inc(mm1_done, 1)

            def turn_q2(t):
                pe.wait_ge(q2_done, t + 1)
                pe.wait_ge(q1T_done, made_q1[0])
                if t:
                    pe.wait_ge(q2T_done, t)
                for k in range(KB):
                    mm = nc.tensor.transpose(tq[:, k * P:(k + 1) * P], q2[:, t % 2, k * P:(k + 1) * P], id_b[:, :])
                mm.then_inc(q2_turned, 1)
                made_q2[0] = t + 1

            def do_mm2(t):
                pe.wait_ge(q2T_done, t + 1)
                pe.wait_ge(x1_half, turned[0])
                if t:
                    pe.wait_ge(res_done, t)
                for k in range(KB):
                    mm = nc.tensor.matmul(mm2, q2T[:, t % 2, k, :], w2q[:, k, :], start=k == 0, stop=k == KB - 1)
                mm.then_inc(mm2_done, 1)
                made[0] = t + 1

            made_q1, made_q2 = [0], [0]
            work = {"convolve": convolve, "wsum": wsum, "xdbl": xdbl, "dtraw": dtraw, "turn_y": turn_y, "turn_q1": turn_q1, "mm1": do_mm1,
                    "turn_q2": turn_q2, "mm2": do_mm2}
            xdbl(0)
            dtraw(0)
            convolve(1)
            pe.wait_ge(in_id, 16)
            for k in range(END):
                if 0 <= k - 1 < UNITS:
                    sum_states(k - 1)
                for name, i in pe_at.get(k, []):
                    work[name](i)

        @block.scalar
        def _(act):
            act.dma_start(inw_sb[:, :], inwT).then_inc(in_inw, 16)
            act.dma_start(taps_sb[:, :, :].rearrange("p s d -> p (s d)"), taps.partition_broadcast(P)).then_inc(in_taps, 16)
            act.dma_start(xproj_sb[:, :, :], xprojT).then_inc(in_proj, 16)
            act.dma_start(dtp_sb[2 * NS:XM, :], dtpT).then_inc(in_dtp, 16)
            act.dma_start(id_f[:, :], ident).then_inc(in_id, 16)

            def silu_u(b):
                if b == 0:
                    act.wait_ge(conv_step, 2 * TAPS)
                    nc.scalar.activation(u[:, :, b, :], cv[:, :, b, :], ACT.Silu).then_inc(u_ready, 1)
                    return
                act.wait_ge(xin_ready, b + 1)
                for h in range(HALVES):
                    ins = nc.scalar.activation(u[:, h, b, :], xin[b][:, h * L:(h + 1) * L], ACT.Silu,
                                               bias=chan_sb[:, h, C_CB:C_CB + 1])
                ins.then_inc(u_ready, 1)

            def copy_xd(b):
                act.wait_ge(xdbl_ready, b + 1)
                nc.scalar.activation(xd[:, b, :], head[0:XM, 0:L], ACT.Copy).then_inc(xd_copied, 1)

            def dt_bias(b):
                act.wait_ge(dtraw_ready, b + 1)
                if b:
                    act.wait_ge(dt_step, 3 * b)
                for h in range(HALVES):
                    nc.scalar.activation(sp_v[:, h, :], head[:, h * L:(h + 1) * L], ACT.Identity,
                                         bias=chan_sb[:, h, C_DTB:C_DTB + 1]).then_inc(dt_v, 1)

            def dt_exp(b):
                act.wait_ge(dt_negd, b + 1)
                nc.scalar.activation(sp_e[:, :, :], sp_e[:, :, :], ACT.Exp).then_inc(dt_e, 1)
                act.wait_ge(dt_e, b + 1)
                nc.scalar.activation(sp_ln[:, :, :], sp_e[:, :, :], ACT.Ln, bias=1.0).then_inc(dt_ln, 1)

            def exps(k):
                b, h, ng = where(k)
                if k == 0:
                    act.wait_ge(negA_ready, 1)
                    act.wait_ge(zeros_set, 1)
                act.wait_ge(dt_step, 3 * b + 2)
                if k >= DA_RING:
                    act.wait_ge(scanned, k - DA_RING + 1)
                for i in range(SG):
                    n = SG * ng + i
                    e = nc.scalar.activation(dA[:, k % DA_RING, i * L + 1:(i + 1) * L], dt[:, h, b % 2, 1:L], ACT.Exp,
                                             scale=negA[:, h, n:n + 1])
                e.then_inc(exp_done, 1)

            def scale_weights(i):
                act.wait_ge(wmean_step, 3)
                nc.scalar.activation(w_raw[:, i], w_raw[:, i], ACT.Identity, bias=ROUND,
                                     scale=wmean[:, i, 1:2]).then_inc(w_scaled, 1)

            def copy_q1(b):
                act.wait_ge(q1_turned, b + 1)
                if b:
                    act.wait_ge(mm1_done, TPB * b)
                nc.scalar.activation(q1T[:, :, :, :].rearrange("p t h n -> p (t h n)"), tq[:, 0:TPB * HALVES * P],
                                     ACT.Copy).then_inc(q1T_done, 1)

            def silu(t):
                i = t % TPB
                act.wait_ge(mm1_done, t + 1)
                if t == 0:
                    act.wait_ge(w_clip, 4)
                if t >= HSLOTS:
                    act.wait_ge(q2_done, t - HSLOTS + 1)
                nc.scalar.activation(hid[:, t % HSLOTS], mm1[i], ACT.Silu, scale=sm1[:, 4, i:i + 1]).then_inc(silu_done, 1)

            def gelu(t):
                act.wait_ge(silu_done, t + 1)
                nc.scalar.activation(hid[:, t % HSLOTS], hid[:, t % HSLOTS], ACT.Gelu).then_inc(gelu_done, 1)

            def norm(t):
                if t >= TILES - TPB:
                    return
                act.wait_ge(root2a_step, 3 * t + 3)
                nc.scalar.activation(hid[:, t % HSLOTS], hid[:, t % HSLOTS], ACT.Identity, bias=sm2[:, t % 2, 2:3],
                                     scale=sm2[:, t % 2, 1:2]).then_inc(norm_done, 1)

            def square(t):
                act.wait_ge(shifted, t + 1)
                if t:
                    act.wait_ge(sq_done, t)
                if t >= 2:
                    act.wait_ge(root2b_step, 2 * (t - 2) + 1)
                nc.scalar.activation(junk[:, :], hid[:, t % HSLOTS], ACT.Square,
                                     accum_out=sm2[:, t % 2, 3:4]).then_inc(sq_done, 1)

            def scale2(t):
                act.wait_ge(sc2_step, 6 * t + 3)
                act.wait_ge(amax2_done, t + 1)
                nc.scalar.activation(hid[:, t % HSLOTS], hid[:, t % HSLOTS], ACT.Identity, bias=ROUND,
                                     scale=sm2[:, t % 2, 8:9]).then_inc(w_done, 1)

            def copy_q2(t):
                act.wait_ge(q2_turned, t + 1)
                if t >= 2:
                    act.wait_ge(mm2_done, t - 1)
                nc.scalar.activation(q2T[:, t % 2].rearrange("p k n -> p (k n)"), tq, ACT.Copy).then_inc(q2T_done, 1)

            def sum_weights(i):
                act.wait_ge((in_w1, in_w2)[i], 16)
                nc.scalar.activation((w1q, w2q)[i][:, :, :].rearrange("p k n -> p (k n)"), w_raw[:, i],
                                     ACT.Abs, accum_out=wabs[:, i:i + 1]).then_inc(wabs_done, 1)

            def silu_z(b):
                act.wait_ge(z_small, 4)
                for h in range(HALVES):
                    j = h * NB + b
                    nc.scalar.activation(siluz[:, h, b, :], x_nat[:, h, b, :], ACT.Silu,
                                         bias=zr[:, 3, j:j + 1], scale=zr[:, 1, j:j + 1]).then_inc(z_ready, 1)

            work = {"silu_u": silu_u, "silu_z": silu_z, "sum_weights": sum_weights, "copy_xd": copy_xd, "dt_bias": dt_bias, "dt_exp": dt_exp,
                    "scale_weights": scale_weights, "copy_q1": copy_q1, "silu": silu, "gelu": gelu, "norm": norm,
                    "square": square, "scale2": scale2, "copy_q2": copy_q2}

            silu_u(0)
            copy_xd(0)
            nc.scalar.preload_act_table_set("natural_log_exp_and_others")
            act.wait_ge(in_chan, 16)
            nc.scalar.activation(negA[:, :, :], chan_sb[:, :, C_A:CH], ACT.Exp).then_inc(expA_done, 1)
            dt_bias(0)
            dt_exp(0)
            for k in range(AHEAD):
                exps(k)
            with_exp = True
            for k in range(END):
                works = [(exps, k + AHEAD)] if k + AHEAD < UNITS else []
                for step, i in works + [(work[name], i) for name, i in act_at.get(k, [])]:
                    if step in (silu_u, silu_z, silu, gelu):
                        with_exp = False
                    elif step in (exps, dt_exp) and not with_exp:
                        nc.scalar.preload_act_table_set("natural_log_exp_and_others")
                        with_exp = True
                    step(i)

        @block.gpsimd
        def _(pool):
            ts, tt = nc.gpsimd.tensor_scalar, nc.gpsimd.tensor_tensor
            nc.gpsimd.memset(ones[:, :], 1.0)
            nc.gpsimd.memset(dA[:, :, :].rearrange("p r (s l) -> p (r s) l", l=L)[:, :, 0:1], 0.0).then_inc(zeros_set, 1)
            nc.gpsimd.memset(m_half[:, :], -0.5).then_inc(consts_set, 1)
            pool.wait_ge(expA_done, 1)
            ts(negA[:, :, :], negA[:, :, :], -1.0, None, ALU.mult).then_inc(negA_ready, 1)

            def z_root():
                pool.wait_ge(z_aggr, HALVES * NB)
                pool.wait_ge(consts_set, 1)
                ts(zr[:, 0, :], zmv[:, :, 1], EPS, None, ALU.add).then_inc(z_small, 1)
                pool.wait_ge(z_small, 1)
                tt(zr[:, 1, :], zr[:, 0, :], m_half[:, :], ALU.pow).then_inc(z_small, 1)
                pool.wait_ge(z_small, 2)
                tt(zr[:, 2, :], zr[:, 1, :], zmv[:, :, 0], ALU.mult).then_inc(z_small, 1)
                pool.wait_ge(z_small, 3)
                ts(zr[:, 3, :], zr[:, 2, :], -1.0, None, ALU.mult).then_inc(z_small, 1)

            def dt_series(b):
                pool.wait_ge(dt_e, b + 1)
                if b:
                    pool.wait_ge(dt_step, 3 * b)
                ts(sp_ser[:, :, :], sp_e[:, :, :], -0.5, 1.0, ALU.mult, ALU.add).then_inc(dt_ser, 1)
                pool.wait_ge(dt_ser, 2 * b + 1)
                tt(sp_ser[:, :, :], sp_ser[:, :, :], sp_e[:, :, :], ALU.mult).then_inc(dt_ser, 1)

            def prod(k):
                b, h, ng = where(k)
                pool.wait_ge(c_in[ng], 16 * (b + 1))
                pool.wait_ge(scanned, k + 1)
                s = st[:, k % ST_RING, :]
                tt(s, s, bc[:, ng, 1].rearrange("p s l -> p (s l)"), ALU.mult).then_inc(prod_done, 1)

            def root1(b):
                pool.wait_ge(mv1_done, TPB * (b + 1))
                if b:
                    pool.wait_ge(sc1_step, 6 * b)
                ts(sm1[:, 0, :], mv1[:, :, 1], 1.0 + EPS, EPS * EPS, ALU.mult, ALU.add).then_inc(root1_step, 1)
                pool.wait_ge(root1_step, 2 * b + 1)
                tt(sm1[:, 1, :], sm1[:, 0, :], m_half[:, 0:TPB], ALU.pow).then_inc(root1_step, 1)

            def add_b2(b):
                pool.wait_ge(xc_done, TPB * (b + 1))
                if b == 0:
                    pool.wait_ge(in_rows, 16)
                tt(x_nat[:, :, b, :], x_nat[:, :, b, :],
                   rows_sb[:, 3 * HID:3 * HID + D].unsqueeze(1).to_broadcast([P, TPB, D]), ALU.add).then_inc(b2_added, 1)

            def root2a(t):
                s = sm2[:, t % 2, :]
                pool.wait_ge(mv2_done, t + 1)
                if t >= 2:
                    pool.wait_ge(norm_done, t - 1)
                ts(s[:, 0:1], mv2[:, t % 2, 1:2], EPS, None, ALU.add).then_inc(root2a_step, 1)
                pool.wait_ge(root2a_step, 3 * t + 1)
                tt(s[:, 1:2], s[:, 0:1], m_half[:, 0:1], ALU.pow).then_inc(root2a_step, 1)
                pool.wait_ge(root2a_step, 3 * t + 2)
                ts(s[:, 2:3], mv2[:, t % 2, 0:1], s[:, 1:2], -1.0, ALU.mult, ALU.mult).then_inc(root2a_step, 1)

            def shift(t):
                if t >= TILES - TPB:
                    return
                h = hid[:, t % HSLOTS]
                pool.wait_ge(gained, t + 1)
                tt(h, h, rows_sb[:, 2 * HID:3 * HID], ALU.add).then_inc(shifted, 1)

            def root2b(t):
                s = sm2[:, t % 2, :]
                pool.wait_ge(sq_done, t + 1)
                if t >= 2:
                    pool.wait_ge(sc2_step, 6 * (t - 1))
                ts(s[:, 4:5], s[:, 3:4], 1.0 / HID, EPS, ALU.mult, ALU.add).then_inc(root2b_step, 1)
                pool.wait_ge(root2b_step, 2 * t + 1)
                tt(s[:, 5:6], s[:, 4:5], m_half[:, 0:1], ALU.pow).then_inc(root2b_step, 1)

            def quant2(t):
                pool.wait_ge(w_done, t + 1)
                if t >= 2:
                    pool.wait_ge(q2_turned, t - 1)
                ts(q2[:, t % 2, :], hid[:, t % HSLOTS], 1.0, -ROUND, ALU.mult, ALU.add).then_inc(q2_done, 1)

            work = {"dt_series": dt_series, "root1": root1, "add_b2": add_b2, "root2a": root2a, "shift": shift,
                    "root2b": root2b, "quant2": quant2}
            z_root()
            for k in range(END):
                if k < UNITS:
                    prod(k)
                for name, i in pool_at.get(k, []):
                    work[name](i)

        @block.vector
        def _(dve):
            ts, tt, stt = nc.vector.tensor_scalar, nc.vector.tensor_tensor, nc.vector.scalar_tensor_tensor

            def conv(b):
                n = 0
                dve.wait_ge(xin_ready, b + 1)
                for s in range(TAPS):
                    for h in range(HALVES):
                        w = chan_sb[:, h, C_CONV + TAPS - 1 - s:C_CONV + TAPS - s]
                        o = cv[:, h, b, :]
                        if s == 0:
                            ins = ts(o, xin[b][:, h * L:(h + 1) * L], w, chan_sb[:, h, C_CB:C_CB + 1], ALU.mult, ALU.add)
                        else:
                            dve.wait_ge(conv_step, n + 2 * (s - 1) + h + 1)
                            ins = stt(out=o[:, s:L], in0=xin[b][:, h * L:(h + 1) * L - s], scalar=w, in1=o[:, s:L],
                                      op0=ALU.mult, op1=ALU.add)
                        ins.then_inc(conv_step, 1)

            def dt_neg(b):
                dve.wait_ge(dt_v, HALVES * (b + 1))
                if b:
                    dve.wait_ge(dt_step, 3 * b)
                stt(out=sp_e[:, :, :], in0=sp_v[:, :, :], scalar=-1.0, in1=sp_v[:, :, :], op0=ALU.mult,
                    op1=ALU.min).then_inc(dt_negd, 1)

            def dt_mask(b):
                dve.wait_ge(dt_e, b + 1)
                ts(sp_mask[:, :, :], sp_e[:, :, :], SMALL_E, None, ALU.is_lt).then_inc(dt_step, 1)
                if b == 0:
                    ts(sp_ser[:, :, :], sp_e[:, :, :], -0.5, 1.0, ALU.mult, ALU.add).then_inc(dt_ser, 1)
                    dve.wait_ge(dt_ser, 1)
                    tt(sp_ser[:, :, :], sp_ser[:, :, :], sp_e[:, :, :], ALU.mult).then_inc(dt_ser, 1)

            def dt_sum(b):
                dve.wait_ge(dt_step, 3 * b + 1)
                dve.wait_ge(dt_ln, b + 1)
                dve.wait_ge(dt_ser, 2 * b + 2)
                flat = "p h l -> p (h l)"
                nc.vector.copy_predicated(sp_ln[:, :, :].rearrange(flat), sp_mask[:, :, :].rearrange(flat).bitcast(I32),
                                          sp_ser[:, :, :].rearrange(flat)).then_inc(dt_cp, 1)
                dve.wait_ge(dt_cp, b + 1)
                if b >= 2:
                    dve.wait_ge(exp_done, UPB * (b - 1))
                    dve.wait_ge(dbu_done, UPB * (b - 1))
                stt(out=dt[:, :, b % 2, :], in0=sp_v[:, :, :], scalar=0.0, in1=sp_ln[:, :, :], op0=ALU.max,
                    op1=ALU.add).then_inc(dt_step, 1)
                dve.wait_ge(dt_step, 3 * b + 2)
                tt(dtu[:, :, b % 2, :], dt[:, :, b % 2, :], u[:, :, b, :], ALU.mult).then_inc(dt_step, 1)

            def mult(k):
                b, h, ng = where(k)
                dve.wait_ge(b_in[ng], 16 * (b + 1))
                if ng == 0 and h == 0:
                    dve.wait_ge(dt_step, 3 * b + 3)
                if k >= DBU_RING:
                    dve.wait_ge(scanned, k - DBU_RING + 1)
                tt(dBu[:, k % DBU_RING, :].rearrange("p (s l) -> p s l", s=SG),
                   dtu[:, h, b % 2, :].unsqueeze(1).to_broadcast([P, SG, L]), bc[:, ng, 0], ALU.mult).then_inc(dbu_done, 1)

            def scan(k):
                dve.wait_ge(dbu_done, k + 1)
                dve.wait_ge(exp_done, k + 1)
                if k >= ST_RING:
                    dve.wait_ge(summed, k - ST_RING + 1)
                nc.vector.tensor_tensor_scan(st[:, k % ST_RING, :], dA[:, k % DA_RING, :], dBu[:, k % DBU_RING, :], 0.0,
                                             ALU.mult, ALU.add).then_inc(scanned, 1)

            def clip_weights(i):
                n = 2 * i
                q = (w1q if i == 0 else w2q)[:, :, :].rearrange("p k n -> p (k n)")
                dve.wait_ge(w_scaled, i + 1)
                ts(w_raw[:, i], w_raw[:, i], ROUND, -1.0, ALU.subtract, ALU.max).then_inc(w_clip, 1)
                dve.wait_ge(w_clip, n + 1)
                ts(q, w_raw[:, i], 1.0, None, ALU.min).then_inc(w_clip, 1)

            def gate(g):
                b, h = g // 2, g % 2
                y = yg[:, g % 2, :]
                dve.wait_ge(summed, GROUPS * (g + 1))
                if g >= 2:
                    dve.wait_ge(y_turned, g - 1)
                stt(out=y, in0=u[:, h, b, :], scalar=chan_sb[:, h, C_D:C_D + 1], in1=yacc, op0=ALU.mult,
                    op1=ALU.add).then_inc(gate_step, 1)
                dve.wait_ge(gate_step, 2 * g + 1)
                dve.wait_ge(z_ready, HALVES * (b + 1))
                tt(y, y, siluz[:, h, b, :], ALU.mult).then_inc(gate_step, 1)

            def add_x1(g):
                b, h = g // 2, g % 2
                dve.wait_ge(y_turned, g + 1)
                tt(x_nat[:, :, b, h * P:(h + 1) * P], x_nat[:, :, b, h * P:(h + 1) * P],
                   yT.rearrange("p (t d) -> p t d", t=TPB), ALU.add).then_inc(x1_half, 1)

            def ln1(b):
                dve.wait_ge(x1_half, 2 * b + 2)
                for i in range(TPB):
                    nc.vector.bn_stats(stats[:, 8 + i, :], x_nat[:, i, b, :]).then_inc(bn1_done, 1)
                if b:
                    dve.wait_ge(root1_step, 2 * b)
                for i in range(TPB):
                    dve.wait_ge(bn1_done, TPB * b + i + 1)
                    nc.vector.bn_aggr(mv1[:, i, :], stats[:, 8 + i, :]).then_inc(mv1_done, 1)
                for i in range(TPB):
                    dve.wait_ge(mv1_done, TPB * b + i + 1)
                    ts(xc[:, i, :], x_nat[:, i, b, :], mv1[:, i, 0:1], None, ALU.subtract).then_inc(xc_done, 1)
                dve.wait_ge(xc_done, TPB * (b + 1))
                nc.vector.tensor_reduce(amax1[:, :], xc[:, :, :], AX.X, ALU.max, apply_absolute_value=True)\
                    .then_inc(amax1_done, 1)

            def quant1(b):
                n, s = 6 * b, [sm1[:, j, :] for j in range(8)]
                dve.wait_ge(amax1_done, b + 1)
                if b:
                    dve.wait_ge(silu_done, TPB * b)
                ts(s[2], amax1[:, :], 1.0 / LEVELS, None, ALU.mult).then_inc(sc1_step, 1)
                dve.wait_ge(sc1_step, n + 1)
                nc.vector.reciprocal(s[5], s[2]).then_inc(sc1_step, 1)
                dve.wait_ge(sc1_step, n + 2)
                dve.wait_ge(root1_step, 2 * b + 2)
                stt(out=s[6], in0=s[1], scalar=LEVELS / EPS, in1=s[5], op0=ALU.mult, op1=ALU.min).then_inc(sc1_step, 1)
                tt(s[3], s[2], s[1], ALU.mult).then_inc(sc1_step, 1)
                dve.wait_ge(sc1_step, n + 4)
                for i in range(TPB):
                    ts(xc[:, i, :], xc[:, i, :], s[6][:, i:i + 1], ROUND, ALU.mult, ALU.add).then_inc(q1_scaled, 1)
                ts(s[4], s[3], EPS / LEVELS, wmean[:, 0, 0:1], ALU.max, ALU.mult).then_inc(sc1_step, 1)
                dve.wait_ge(q1_scaled, TPB * (b + 1))
                if b:
                    dve.wait_ge(q1_turned, b)
                ts(q1[:, :, :], xc[:, :, :], ROUND, None, ALU.subtract).then_inc(q1_done, 1)
                dve.wait_ge(sc1_step, n + 5)
                nc.vector.reciprocal(s[7], s[4]).then_inc(sc1_step, 1)
                dve.wait_ge(sc1_step, n + 6)
                if b:
                    dve.wait_ge(mm1_done, TPB * b)
                for i in range(TPB):
                    ts(diag[:, i, :], id_f[:, :], s[7][:, i:i + 1], None, ALU.mult).then_inc(diag_done, 1)

            def bn2(t):
                dve.wait_ge(gelu_done, t + 1)
                o = 10 + 2 * (t % 2)
                for i in range(2):
                    nc.vector.bn_stats(stats[:, o + i, :], hid[:, t % HSLOTS, 512 * i:512 * (i + 1)]).then_inc(bn2_done, 1)
                dve.wait_ge(bn2_done, 2 * t + 2)
                if t >= 2:
                    dve.wait_ge(root2a_step, 3 * (t - 1))
                nc.vector.bn_aggr(mv2[:, t % 2, :], stats[:, o:o + 2, :].rearrange("p a b -> p (a b)")).then_inc(mv2_done, 1)

            def gain(t):
                h = hid[:, t % HSLOTS]
                if t >= TILES - TPB:
                    dve.wait_ge(mv2_done, t + 1)
                    stt(out=h, in0=h, scalar=mv2[:, t % 2, 0:1], in1=rows_sb[:, HID:2 * HID], op0=ALU.subtract,
                        op1=ALU.mult).then_inc(gained, 1)
                    dve.wait_ge(root2a_step, 3 * t + 2)
                    dve.wait_ge(gained, t + 1)
                    stt(out=h, in0=h, scalar=sm2[:, t % 2, 1:2], in1=rows_sb[:, 2 * HID:3 * HID], op0=ALU.mult,
                        op1=ALU.add).then_inc(shifted, 1)
                    return
                dve.wait_ge(norm_done, t + 1)
                tt(h, h, rows_sb[:, HID:2 * HID], ALU.mult).then_inc(gained, 1)

            def do_amax2(t):
                dve.wait_ge(shifted, t + 1)
                if t >= 2:
                    dve.wait_ge(sc2_step, 6 * (t - 1))
                nc.vector.tensor_reduce(am2[:, t % 2:t % 2 + 1], hid[:, t % HSLOTS], AX.X, ALU.max,
                                        apply_absolute_value=True).then_inc(amax2_done, 1)

            def scales2(t):
                n, s = 6 * t, [sm2[:, t % 2, j:j + 1] for j in range(12)]
                dve.wait_ge(amax2_done, t + 1)
                if t >= 2:
                    dve.wait_ge(w_done, t - 1)
                    dve.wait_ge(res_done, t - 1)
                ts(s[6], am2[:, t % 2:t % 2 + 1], 1.0 / LEVELS, None, ALU.mult).then_inc(sc2_step, 1)
                dve.wait_ge(sc2_step, n + 1)
                nc.vector.reciprocal(s[7], s[6]).then_inc(sc2_step, 1)
                dve.wait_ge(sc2_step, n + 2)
                dve.wait_ge(root2b_step, 2 * t + 2)
                stt(out=s[8], in0=s[5], scalar=LEVELS / EPS, in1=s[7], op0=ALU.mult, op1=ALU.min).then_inc(sc2_step, 1)
                tt(s[9], s[6], s[5], ALU.mult).then_inc(sc2_step, 1)
                dve.wait_ge(sc2_step, n + 4)
                ts(s[10], s[9], EPS / LEVELS, wmean[:, 1, 0:1], ALU.max, ALU.mult).then_inc(sc2_step, 1)
                dve.wait_ge(sc2_step, n + 5)
                dve.sem_inc(sc2_step, 1)

            def quant2(t):
                dve.wait_ge(w_done, t + 1)
                dve.wait_ge(q2_turned, t - 1)
                ts(q2[:, t % 2, :], hid[:, t % HSLOTS], ROUND, None, ALU.subtract).then_inc(q2_done, 1)

            def result(t):
                b, i = t // TPB, t % TPB
                dve.wait_ge(mm2_done, t + 1)
                dve.wait_ge(b2_added, b + 1)
                if t >= 2:
                    dve.wait_ge(out_done[t % 2], 16 * (t // 2))
                stt(out=res[:, t % 2, :], in0=mm2, scalar=sm2[:, t % 2, 10:11], in1=x_nat[:, i, b, :],
                    op0=ALU.mult, op1=ALU.add).then_inc(res_done, 1)

            def z_norm():
                dve.wait_ge(in_x, 16 * HALVES)
                for j in range(HALVES * NB):
                    nc.vector.bn_stats(stats[:, j, :], x_nat[:, j // NB, j % NB, :]).then_inc(z_stats, 1)
                for j in range(HALVES * NB):
                    dve.wait_ge(z_stats, j + 1)
                    nc.vector.bn_aggr(zmv[:, j, :], stats[:, j, :]).then_inc(z_aggr, 1)

            def mean_weights(_):
                dve.wait_ge(wsum_ready, 1)
                for i in range(2):
                    ts(wmean[:, i, 0:1], bank(6)[:, i:i + 1], 1.0 / (HID * D), EPS, ALU.mult, ALU.max)\
                        .then_inc(wmean_step, 1)
                dve.wait_ge(wmean_step, 2)
                nc.vector.reciprocal(wmean[:, :, 1], wmean[:, :, 0]).then_inc(wmean_step, 1)

            dve.wait_ge(in_chan, 16)
            conv(0)
            dve.wait_ge(in_taps, 16)
            dve.wait_ge(in_inw, 16)
            tt(inw_taps[:, :, :], taps_sb[:, :, :], inw_sb[:, :].unsqueeze(1).to_broadcast([P, TAPS, D]), ALU.mult)\
                .then_inc(taps_scaled, 1)
            z_norm()
            dt_neg(0)
            dve.wait_ge(in_id, 16)
            nc.vector.tensor_copy(id_b[:, :], id_f[:, :]).then_inc(id_cast, 1)
            dt_mask(0)
            dt_sum(0)
            mult(0)
            work = {"wmean": mean_weights, "conv": conv, "dt_neg": dt_neg, "dt_mask": dt_mask, "dt_sum": dt_sum, "clip_weights": clip_weights,
                    "gate": gate, "x1": add_x1, "ln1": ln1, "quant1": quant1, "bn2": bn2, "gain": gain,
                    "amax2": do_amax2, "scales2": scales2, "quant2": quant2, "res": result}
            for k in range(END):
                if k + 1 < UNITS:
                    mult(k + 1)
                if k < UNITS:
                    scan(k)
                for name, i in vec_at.get(k, []):
                    work[name](i)


def kernel(x, ctx_1024, L0_xattn_in_proj_w, L0_xattn_conv_w, L0_xattn_conv_b, L0_xattn_x_proj_w,
           L0_xattn_dt_proj_w, L0_xattn_dt_proj_b, L0_xattn_A_log, L0_xattn_D, L0_ffn_w1, L0_ffn_b1,
           L0_ffn_ln_g, L0_ffn_ln_b, L0_ffn_w2, L0_ffn_b2):
    import numpy as np
    import concourse.bacc as bacc
    from concourse.bass_utils import run_bass_kernel_spmd

    def halves(a):
        return np.ascontiguousarray(a.reshape(HALVES, P, -1).transpose(1, 0, 2))

    f = np.asarray
    xp = f(L0_xattn_x_proj_w)
    bcw = xp[R:].reshape(2, GROUPS, SG, D).transpose(1, 0, 2, 3).reshape(2 * NS, D)
    chan = np.concatenate([f(L0_xattn_conv_w)[:, 0, :], f(L0_xattn_conv_b)[:, None], f(L0_xattn_dt_proj_b)[:, None],
                           f(L0_xattn_D)[:, None], f(L0_xattn_A_log)], axis=1)
    data = {
        "x": np.ascontiguousarray(f(x)),
        "ctxT": np.ascontiguousarray(f(ctx_1024).reshape(NB * L, DM).T),
        "inwT": np.ascontiguousarray(f(L0_xattn_in_proj_w).T),
        "xprojT": halves(np.concatenate([bcw, xp[:R]], axis=0).T),
        "dtpT": np.ascontiguousarray(f(L0_xattn_dt_proj_w).T),
        "chan": halves(chan),
        "taps": np.ascontiguousarray(f(L0_xattn_conv_w)[:, 0, ::-1].T).reshape(TAPS * D),
        "w1T": np.ascontiguousarray(f(L0_ffn_w1).T),
        "w2T": np.ascontiguousarray(f(L0_ffn_w2).T),
        "rows": np.concatenate([f(L0_ffn_b1), f(L0_ffn_ln_g), f(L0_ffn_ln_b), f(L0_ffn_b2)]),
        "ident": np.eye(P, dtype=np.float32),
    }
    nc = bacc.Bacc("TRN2", target_bir_lowering=False, num_devices=1)
    args = [nc.dram_tensor(n, a.shape, mybir.dt.from_np(a.dtype), kind="ExternalInput").ap() for n, a in data.items()]
    spread = nc.dram_tensor("spread", (NB, 2 * NS, L), F32, kind="Internal").ap()
    out = nc.dram_tensor("out", (NB, L, D), F32, kind="ExternalOutput").ap()
    mixer_ffn(nc, *args, spread, out)
    r = run_bass_kernel_spmd(nc, [data], core_ids=[0])
    return r.results[0]["out"]
```

```python
from contextlib import ExitStack

import concourse.bass as bass
from concourse import mybir

F32 = mybir.dt.float32
BF16 = mybir.dt.bfloat16
I32 = mybir.dt.int32
ACT = mybir.ActivationFunctionType
ALU = mybir.AluOpType
AX = mybir.AxisListType

P = 128
NB, L, D = 4, 256, 256
DM = 128
NS, R, TAPS = 16, 8, 4
HID = 1024
HALVES = D // P
SG = 4
GROUPS = NS // SG
UPB = HALVES * GROUPS
UNITS = NB * UPB
UW = SG * L
DA_RING, DBU_RING, ST_RING = 6, 2, 6
AHEAD = 2
TPB = L // P
TILES = NB * TPB
KB = HID // P
HSLOTS = 4
EPS = 1e-5
LEVELS = 127.0
ROUND = 12582912.0
SMALL_E = 2.0 ** -8
C_CONV, C_CB, C_DTB, C_D, C_A = 0, TAPS, TAPS + 1, TAPS + 2, TAPS + 3
CH = C_A + NS
XM = 2 * NS + R


STEPS = ("ln1", "root1", "quant1", "turn_q1", "add_b2", "copy_q1", "mm1", "silu", "gelu", "bn2", "root2a", "norm",
         "gain", "shift", "amax2", "square", "root2b", "scales2", "scale2", "quant2", "turn_q2", "copy_q2", "mm2", "res")
LAGS = ((2, 2, 3, 3, 5, 3, 4, 6, 6, 8, 8, 8, 10, 10, 12, 11, 11, 12, 13, 13, 13, 14, 15, 16),
        (2, 2, 3, 3, 5, 3, 4, 6, 6, 8, 8, 8, 10, 10, 12, 11, 11, 12, 13, 13, 13, 14, 15, 16),
        (2, 2, 3, 4, 4, 4, 4, 5, 5, 6, 6, 7, 7, 8, 11, 11, 11, 12, 12, 12, 13, 13, 14, 15),
        (2, 2, 2, 2, 5, 3, 3, 4, 4, 6, 6, 7, 6, 6, 7, 7, 7, 7, 7, 8, 8, 8, 8, 10))
APARTS = ((0, 0, 0, 0, 0, 0, 0, 0, 0, 0, 0, 0, 1, 1, 1, 1, 1, 1, 1, 1, 1, 1, 1, 1),
          (0, 0, 0, 0, 0, 0, 0, 0, 0, 0, 0, 0, 1, 1, 1, 1, 1, 1, 1, 1, 1, 1, 1, 1),
          (0, 0, 0, 0, 0, 0, 0, 0, 0, 0, 0, 0, 0, 0, 0, 0, 0, 0, 0, 0, 1, 1, 2, 2),
          (0, 0, 0, 0, 0, 0, 0, 1, 1, 1, 2, 0, 2, 2, 2, 1, 1, 2, 2, 1, 1, 1, 1, 1))
GATES = ((1, 1, 2), (1, 1, 2))
DTLAGS = ({"xdbl": 0, "copy_xd": 0, "dtraw": 0, "dt_bias": 1, "dt_neg": 2, "dt_exp": 2, "dt_series": 2, "dt_mask": 3,
           "dt_sum": 4},
          {"xdbl": -1, "copy_xd": -1, "dtraw": 0, "dt_bias": 0, "dt_neg": 2, "dt_exp": 2, "dt_series": 3, "dt_mask": 3,
           "dt_sum": 4})
EARLY = {("dt_half", 1): 0, ("convolve", 2): 0, ("convolve", 3): 2, ("silu_u", 1): 0, ("silu_u", 2): 4,
         ("silu_u", 3): 4, ("silu_z", 0): 4, ("silu_z", 1): 4, ("silu_z", 2): 14, ("silu_z", 3): 16,
         ("sum_weights", 0): 6, ("sum_weights", 1): 7, ("wsum", 0): 8, ("wmean", 0): 10, ("scale_weights", 0): 10,
         ("scale_weights", 1): 10, ("clip_weights", 0): 11, ("clip_weights", 1): 12}
VECTOR = ("dt_half", "wmean", "clip_weights", "dt_neg", "dt_mask", "dt_sum", "ln1", "quant1", "bn2", "gain", "amax2",
          "scales2", "res")
SCALAR = ("silu_u", "sum_weights", "silu_z", "scale_weights", "copy_xd", "dt_bias", "dt_exp", "copy_q1", "silu",
          "gelu", "norm", "square", "scale2", "copy_q2")
POOL = ("dt_series", "root1", "add_b2", "root2a", "shift", "root2b", "out_scale", "quant2")
PER_TILE = STEPS[STEPS.index("mm1"):]


def schedule():
    vec, act, pool, pe = {}, {}, {}, {}

    def put(table, at, *work):
        table.setdefault(at, []).append(work)

    def place(step, at, i):
        last = step == "quant2" and i >= TILES - TPB
        table = vec if step in VECTOR or last else act if step in SCALAR else pool if step in POOL else pe
        put(table, at, step, i)

    for (step, i), at in EARLY.items():
        place(step, at, i)
    for b in range(1, NB):
        for step, lag in DTLAGS[min(b, 2) - 1].items():
            place(step, UPB * (b - 1) + lag, b)
    for b in range(NB):
        for h in range(HALVES):
            e = UPB * b + GROUPS * (h + 1)
            for table, step, lag in zip((vec, pe, vec), ("gate", "turn_y", "x1"), GATES[e == UNITS]):
                put(table, e + lag, step, 2 * b + h)
        e = UPB * (b + 1)
        for step, lag, apart in zip(STEPS, LAGS[b], APARTS[b]):
            if step in PER_TILE:
                for i in range(TPB):
                    place(step, e + lag + i * apart, TPB * b + i)
                    if step == "res":
                        place("out_scale", e + lag + i * apart - 1, TPB * b + i)
            else:
                place(step, e + lag, b)
    order = {"gate": -3, "turn_y": -2, "x1": -1}
    for table in (vec, pe):
        for works in table.values():
            works.sort(key=lambda w: order.get(w[0], 0))
    return vec, act, pool, pe, UNITS + max(LAGS[-1]) + 2


def mixer_ffn(nc, x, ctxT, inwT, xprojT, dtpT, chan, taps, w1T, w2T, rows, ident, spread, out):
    vec_at, act_at, pool_at, pe_at, END = schedule()
    with ExitStack() as ctx:
        def sb(name, shape, dt=F32):
            return ctx.enter_context(nc.sbuf_tensor(name, shape, dt))

        def sem(name):
            return ctx.enter_context(nc.semaphore(name))

        x_nat = sb("x_nat", [P, HALVES, NB, D])
        siluz = sb("siluz", [P, HALVES, NB, L])
        ctx_sb = sb("ctx_sb", [P, NB * L])
        inw_sb = sb("inw_sb", [P, D])
        taps_sb = sb("taps_sb", [P, TAPS, D])
        inw_taps = taps_sb
        xproj_sb = sb("xproj_sb", [P, HALVES, XM])
        dtp_sb = sb("dtp_sb", [XM, D])
        chan_sb = sb("chan_sb", [P, HALVES, CH])
        id_f = sb("id_f", [P, P])
        id_b = sb("id_b", [P, P], BF16)
        ones = sb("ones", [P, P])
        diag_D = sb("diag_D", [P, HALVES, P])
        cv = sb("cv", [P, HALVES, NB, L])
        u = cv
        dt = sb("dt", [P, HALVES, 2, L])
        dtu = sb("dtu", [P, HALVES, 2, L])
        negA = sb("negA", [P, HALVES, NS])
        xd = sb("xd", [XM, NB, L])
        sp_v, sp_e, sp_ln, sp_mask, sp_ser = (sb(n, [P, HALVES, L]) for n in ("sp_v", "sp_e", "sp_ln", "sp_mask", "sp_ser"))
        bc = sb("bc", [P, GROUPS, 2, SG, L])
        dA = sb("dA", [P, DA_RING, UW])
        dBu = sb("dBu", [P, DBU_RING, UW])
        st = sb("st", [P, ST_RING, UW])
        yg = sb("yg", [P, 2, L])
        w1q = sb("w1q", [P, HALVES, HID], BF16)
        w2q = sb("w2q", [P, KB, D], BF16)
        rows_sb = sb("rows_sb", [P, 3 * HID + D])
        w_raw = sb("w_raw", [P, 2, 2048])
        hid = w_raw[:, :, :].rearrange("p a (b n) -> p (a b) n", b=2)
        xc = sb("xc", [P, TPB, D])
        q1 = sb("q1", [P, TPB, D], BF16)
        q1T = sb("q1T", [P, TPB, HALVES, P], BF16)
        diag = sb("diag", [P, 2, P])
        q2 = sb("q2", [P, 2, HID], BF16)
        q2T = sb("q2T", [P, 2, KB, P], BF16)
        junk = sb("junk", [P, HID], BF16)
        res = sb("res", [P, 2, D])
        stats = sb("stats", [P, 8 + 2 + 4, 6])
        zmv = sb("zmv", [P, HALVES * NB, 2])
        zr = sb("zr", [P, 4, HALVES * NB])
        mv1 = sb("mv1", [P, TPB, 2])
        amax1 = sb("amax1", [P, TPB])
        sm1 = sb("sm1", [P, 8, TPB])
        mv2 = sb("mv2", [P, 2, 2])
        am2 = sb("am2", [P, 2])
        sm2 = sb("sm2", [P, 2, 16])
        wabs = sb("wabs", [P, 2])
        wmean = sb("wmean", [P, 2, 3])
        m_half = sb("m_half", [P, 8])

        ps = ctx.enter_context(nc.psum_tensor("ps", [P, 8 * 512], F32))

        def bank(n, k=1):
            return ps[:, n * 512:(n + k) * 512]

        yacc = bank(0)[:, 0:L]
        head = bank(1)
        mm2, yT = bank(2)[:, 0:D], bank(2)[:, D:2 * D]
        tq = bank(3).bitcast(BF16)
        mm1 = [bank(4, 2), bank(6, 2)]
        xin = [bank(1), bank(7), bank(4), bank(5)]

        def raw(b, h):
            return bank(6)[:, 0:L] if b == 0 and h else head[:, h * L:(h + 1) * L]

        in_ctx0, in_ctx, in_inw, in_chan, in_taps, in_x, in_proj, in_dtp, in_id, in_w1, in_w2, in_rows = (
            sem("in_" + n) for n in ("ctx0", "ctx", "inw", "chan", "taps", "x", "proj", "dtp", "id", "w1", "w2", "rows"))
        spread_out = sem("spread_out")
        b_in, c_in = ([sem(f"{n}_in{g}") for g in range(GROUPS)] for n in "bc")
        out_done = [sem("out_done_even"), sem("out_done_odd")]
        consts_set, zeros_set, id_cast = sem("consts_set"), sem("zeros_set"), sem("id_cast")
        z_stats, z_aggr, z_small, z_ready = sem("z_stats"), sem("z_aggr"), sem("z_small"), sem("z_ready")
        expA_done, negA_ready = sem("expA_done"), sem("negA_ready")
        wabs_done, wsum_ready, wmean_step = sem("wabs_done"), sem("wsum_ready"), sem("wmean_step")
        w_scaled, w_clip = sem("w_scaled"), sem("w_clip")
        taps_scaled, diag_D_done = sem("taps_scaled"), sem("diag_D_done")
        xin_ready, conv_step, u_ready = sem("xin_ready"), sem("conv_step"), sem("u_ready")
        xdbl_ready, xd_copied, dtraw_ready = sem("xdbl_ready"), sem("xd_copied"), sem("dtraw_ready")
        dt_v, dt_negd, dt_e, dt_ln = sem("dt_v"), sem("dt_negd"), sem("dt_e"), sem("dt_ln")
        dt_ser, dt_step, dt_cp = sem("dt_ser"), sem("dt_step"), sem("dt_cp")
        dbu_done, exp_done, scanned, prod_done, summed = (
            sem(n) for n in ("dbu_done", "exp_done", "scanned", "prod_done", "summed"))
        gate_step, y_turned, x1_half = sem("gate_step"), sem("y_turned"), sem("x1_half")
        bn1_done, mv1_done, xc_done, amax1_done, root1_step, sc1_step = (
            sem(n) for n in ("bn1_done", "mv1_done", "xc_done", "amax1_done", "root1_step", "sc1_step"))
        q1_scaled, q1_done, q1_turned, q1T_done, b2_added = (
            sem(n) for n in ("q1_scaled", "q1_done", "q1_turned", "q1T_done", "b2_added"))
        diag_done, mm1_done, silu_done, gelu_done, bn2_done, mv2_done, root2a_step, norm_done, gained, shifted = (
            sem(n) for n in ("diag_done", "mm1_done", "silu_done", "gelu_done", "bn2_done", "mv2_done",
                             "root2a_step", "norm_done", "gained", "shifted"))
        amax2_done, sq_done, root2b_step, sc2_step, out_scaled, w_done, q2_done, q2_turned, q2T_done, mm2_done, res_done = (
            sem(n) for n in ("amax2_done", "sq_done", "root2b_step", "sc2_step", "out_scaled", "w_done", "q2_done",
                             "q2_turned", "q2T_done", "mm2_done", "res_done"))

        def where(k):
            return k // UPB, k // GROUPS % HALVES, k % GROUPS

        def parts_before(b):
            return b + 1 if b else 0

        def parts(b):
            return [(parts_before(b), slice(0, HALVES))] if b else [(h, slice(h, h + 1)) for h in range(HALVES)]

        block = ctx.enter_context(nc.Block())

        @block.sync
        def _(sp):
            sp.dma_start(ctx_sb[:, 0:L], ctxT[:, 0:L]).then_inc(in_ctx0, 16)
            sp.dma_start(chan_sb[:, :, :], chan).then_inc(in_chan, 16)
            sp.dma_start(ctx_sb[:, L:NB * L], ctxT[:, L:NB * L]).then_inc(in_ctx, 16)
            for h in range(HALVES):
                sp.dma_start(x_nat[:, h], x[:, h * P:(h + 1) * P, :].rearrange("b p d -> p b d")).then_inc(in_x, 16)

            def store(t):
                sp.wait_ge(res_done, t + 1)
                sp.dma_start(out[t // TPB, t % TPB * P:(t % TPB + 1) * P, :], res[:, t % 2, :])\
                    .then_inc(out_done[t % 2], 16)

            for b in range(NB):
                sp.wait_ge(xd_copied, b + 1)
                sp.dma_start(spread[b], xd[0:2 * NS, b, :]).then_inc(spread_out, 16)
                sp.wait_ge(spread_out, 16 * (b + 1))

                def load(g, c):
                    if b:
                        sp.wait_ge((dbu_done, prod_done)[c], UPB * b - GROUPS + g + 1)
                    r = SG * (2 * g + c)
                    sp.dma_start(bc[:, g, c].rearrange("p s l -> p (s l)"),
                                 spread[b, r:r + SG, :].rearrange("s l -> (s l)").partition_broadcast(P))\
                        .then_inc((b_in, c_in)[c][g], 16)

                load(0, 0)
                for g in range(GROUPS):
                    if g + 1 < GROUPS:
                        load(g + 1, 0)
                    load(g, 1)
                if b == 0:
                    sp.dma_start(w_raw[:, 0].rearrange("p (k n) -> p k n", k=HALVES),
                                 w1T.rearrange("(k p) n -> p k n", p=P)).then_inc(in_w1, 16)
                    sp.dma_start(w_raw[:, 1].rearrange("p (k n) -> p k n", k=KB),
                                 w2T.rearrange("(k p) n -> p k n", p=P)).then_inc(in_w2, 16)
                    sp.dma_start(rows_sb[:, :], rows.partition_broadcast(P)).then_inc(in_rows, 16)
            for t in range(TILES):
                store(t)
            for s in out_done:
                sp.wait_ge(s, 16 * TILES // 2)

        @block.tensor
        def _(pe):
            turned, made = [0], [0]

            pe.wait_ge(in_inw, 16)
            pe.wait_ge(in_ctx0, 16)
            for h in range(HALVES):
                mm = nc.tensor.matmul(xin[0][:, h * L:(h + 1) * L], inw_sb[:, h * P:(h + 1) * P], ctx_sb[:, 0:L],
                                      start=True, stop=True)
            mm.then_inc(xin_ready, 1)

            def convolve(b):
                pe.wait_ge(in_ctx, 16)
                pe.wait_ge(taps_scaled, 1)
                for h in range(HALVES):
                    for s in range(TAPS):
                        mm = nc.tensor.matmul(xin[b][:, h * L + s:(h + 1) * L], inw_taps[:, s, h * P:(h + 1) * P],
                                              ctx_sb[:, b * L:(b + 1) * L - s], start=s == 0, stop=s == TAPS - 1)
                mm.then_inc(xin_ready, 1)

            def xdbl(b):
                if b == 0:
                    pe.wait_ge(in_proj, 16)
                else:
                    pe.wait_ge(dt_v, HALVES * b)
                pe.wait_ge(u_ready, b + 1)
                for h in range(HALVES):
                    mm = nc.tensor.matmul(head[0:XM, 0:L], xproj_sb[:, h, :], u[:, h, b, :], start=h == 0, stop=h == 1)
                mm.then_inc(xdbl_ready, 1)

            def dtraw(b):
                if b == 0:
                    pe.wait_ge(in_dtp, 16)
                pe.wait_ge(xd_copied, b + 1)
                for h in range(HALVES):
                    mm = nc.tensor.matmul(raw(b, h), dtp_sb[2 * NS:XM, h * P:(h + 1) * P],
                                          xd[2 * NS:XM, b, :], start=True, stop=True)
                    if b == 0:
                        mm.then_inc(dtraw_ready, 1)
                if b:
                    mm.then_inc(dtraw_ready, 1)

            def sum_states(k):
                b, h, ng = where(k)
                if ng == 0:
                    if k == 0:
                        pe.wait_ge(diag_D_done, HALVES)
                    else:
                        pe.wait_ge(gate_step, k // GROUPS)
                    pe.wait_ge(u_ready, b + 1)
                    nc.tensor.matmul(yacc, diag_D[:, h, :], u[:, h, b, :], start=True, stop=False)
                pe.wait_ge(prod_done, k + 1)
                for i in range(SG):
                    mm = nc.tensor.matmul(yacc, id_f[:, :], st[:, k % ST_RING, i * L:(i + 1) * L], start=False,
                                          stop=ng == GROUPS - 1 and i == SG - 1)
                mm.then_inc(summed, 1)

            def wsum(_):
                pe.wait_ge(wabs_done, 2)
                pe.wait_ge(consts_set, 1)
                nc.tensor.matmul(bank(6)[:, 0:2], ones[:, :], wabs[:, :], start=True, stop=True).then_inc(wsum_ready, 1)

            def turn_y(g):
                pe.wait_ge(gate_step, g + 1)
                if g:
                    pe.wait_ge(x1_half, g)
                if made[0]:
                    pe.wait_ge(res_done, made[0])
                for i in range(TPB):
                    mm = nc.tensor.transpose(yT[:, i * P:(i + 1) * P], yg[:, g % 2, i * P:(i + 1) * P], id_f[:, :])
                mm.then_inc(y_turned, 1)
                turned[0] = g + 1

            def turn_q1(b):
                pe.wait_ge(q1_done, b + 1)
                if b == 0:
                    pe.wait_ge(id_cast, 1)
                else:
                    pe.wait_ge(q2T_done, made_q2[0])
                for t in range(TPB):
                    for h in range(HALVES):
                        o = (t * HALVES + h) * P
                        mm = nc.tensor.transpose(tq[:, o:o + P], q1[:, t, h * P:(h + 1) * P], id_b[:, :])
                mm.then_inc(q1_turned, 1)
                made_q1[0] = b + 1

            def do_mm1(t):
                b, i = t // TPB, t % TPB
                pe.wait_ge(diag_done, t + 1)
                if t == 0:
                    pe.wait_ge(in_rows, 16)
                    pe.wait_ge(w_clip, 4)
                    pe.wait_ge(u_ready, NB)
                if b:
                    pe.wait_ge(silu_done, t - 1)
                cols = [slice(n * 512, (n + 1) * 512) for n in range(2)]
                for c in cols:
                    nc.tensor.matmul(mm1[i][:, c], diag[:, i, :], rows_sb[:, c], start=True, stop=False)
                pe.wait_ge(q1T_done, b + 1)
                for c in cols:
                    for k in range(HALVES):
                        mm = nc.tensor.matmul(mm1[i][:, c], q1T[:, i, k, :], w1q[:, k, c], start=False, stop=k == 1)
                mm.then_inc(mm1_done, 1)

            def turn_q2(t):
                pe.wait_ge(q2_done, t + 1)
                pe.wait_ge(q1T_done, made_q1[0])
                if t:
                    pe.wait_ge(q2T_done, t)
                for k in range(KB):
                    mm = nc.tensor.transpose(tq[:, k * P:(k + 1) * P], q2[:, t % 2, k * P:(k + 1) * P], id_b[:, :])
                mm.then_inc(q2_turned, 1)
                made_q2[0] = t + 1

            def do_mm2(t):
                pe.wait_ge(q2T_done, t + 1)
                pe.wait_ge(x1_half, turned[0])
                if t:
                    pe.wait_ge(res_done, t)
                for k in range(KB):
                    mm = nc.tensor.matmul(mm2, q2T[:, t % 2, k, :], w2q[:, k, :], start=k == 0, stop=k == KB - 1)
                mm.then_inc(mm2_done, 1)
                made[0] = t + 1

            made_q1, made_q2 = [0], [0]
            work = {"convolve": convolve, "wsum": wsum, "xdbl": xdbl, "dtraw": dtraw, "turn_q1": turn_q1, "mm1": do_mm1,
                    "turn_q2": turn_q2, "mm2": do_mm2}
            xdbl(0)
            dtraw(0)
            convolve(1)
            pe.wait_ge(in_id, 16)
            for k in range(END):
                works = pe_at.get(k, [])
                for name, i in works:
                    if name == "turn_y":
                        turn_y(i)
                if 0 <= k - 1 < UNITS:
                    sum_states(k - 1)
                for name, i in works:
                    if name != "turn_y":
                        work[name](i)

        @block.scalar
        def _(act):
            act.dma_start(inw_sb[:, :], inwT).then_inc(in_inw, 16)
            act.dma_start(taps_sb[:, :, :].rearrange("p s d -> p (s d)"), taps.partition_broadcast(P)).then_inc(in_taps, 16)
            act.dma_start(xproj_sb[:, :, :], xprojT).then_inc(in_proj, 16)
            act.dma_start(dtp_sb[2 * NS:XM, :], dtpT).then_inc(in_dtp, 16)
            act.dma_start(id_f[:, :], ident).then_inc(in_id, 16)

            def silu_u(b):
                if b == 0:
                    act.wait_ge(conv_step, 2 * TAPS)
                    nc.scalar.activation(u[:, :, b, :], cv[:, :, b, :], ACT.Silu).then_inc(u_ready, 1)
                    return
                act.wait_ge(xin_ready, b + 1)
                for h in range(HALVES):
                    ins = nc.scalar.activation(u[:, h, b, :], xin[b][:, h * L:(h + 1) * L], ACT.Silu,
                                               bias=chan_sb[:, h, C_CB:C_CB + 1])
                ins.then_inc(u_ready, 1)

            def copy_xd(b):
                act.wait_ge(xdbl_ready, b + 1)
                nc.scalar.activation(xd[:, b, :], head[0:XM, 0:L], ACT.Copy).then_inc(xd_copied, 1)

            def dt_bias(b):
                if b:
                    act.wait_ge(dt_step, 3 * parts_before(b))
                for h in range(HALVES):
                    act.wait_ge(dtraw_ready, parts_before(b) + 1 + (h if b == 0 else 0))
                    nc.scalar.activation(sp_v[:, h, :], raw(b, h), ACT.Identity,
                                         bias=chan_sb[:, h, C_DTB:C_DTB + 1]).then_inc(dt_v, 1)

            def dt_exp(b):
                for n, hs in parts(b):
                    act.wait_ge(dt_negd, n + 1)
                    nc.scalar.activation(sp_e[:, hs, :], sp_e[:, hs, :], ACT.Exp).then_inc(dt_e, 1)
                    act.wait_ge(dt_e, n + 1)
                    nc.scalar.activation(sp_ln[:, hs, :], sp_e[:, hs, :], ACT.Ln, bias=1.0).then_inc(dt_ln, 1)

            def exps(k):
                b, h, ng = where(k)
                if k == 0:
                    act.wait_ge(negA_ready, 1)
                    act.wait_ge(zeros_set, 1)
                act.wait_ge(dt_step, 3 * (parts_before(b) if b else h) + 2)
                if k >= DA_RING:
                    act.wait_ge(scanned, k - DA_RING + 1)
                for i in range(SG):
                    n = SG * ng + i
                    e = nc.scalar.activation(dA[:, k % DA_RING, i * L + 1:(i + 1) * L], dt[:, h, b % 2, 1:L], ACT.Exp,
                                             scale=negA[:, h, n:n + 1])
                e.then_inc(exp_done, 1)

            def scale_weights(i):
                act.wait_ge(wmean_step, 4)
                nc.scalar.activation(w_raw[:, i], w_raw[:, i], ACT.Identity, bias=ROUND,
                                     scale=wmean[:, i, 1:2]).then_inc(w_scaled, 1)

            def copy_q1(b):
                if b == NB - 1:
                    nc.scalar.preload_act_table_set("silu_and_others")
                act.wait_ge(q1_turned, b + 1)
                if b:
                    act.wait_ge(mm1_done, TPB * b)
                nc.scalar.activation(q1T[:, :, :, :].rearrange("p t h n -> p (t h n)"), tq[:, 0:TPB * HALVES * P],
                                     ACT.Copy).then_inc(q1T_done, 1)

            def silu(t):
                i = t % TPB
                act.wait_ge(mm1_done, t + 1)
                if t == 0:
                    act.wait_ge(w_clip, 4)
                if t >= HSLOTS:
                    act.wait_ge(q2_done, t - HSLOTS + 1)
                nc.scalar.activation(hid[:, t % HSLOTS], mm1[i], ACT.Silu, scale=sm1[:, 4, i:i + 1]).then_inc(silu_done, 1)

            def gelu(t):
                act.wait_ge(silu_done, t + 1)
                nc.scalar.activation(hid[:, t % HSLOTS], hid[:, t % HSLOTS], ACT.Gelu).then_inc(gelu_done, 1)

            def norm(t):
                if t >= TILES - TPB:
                    return
                act.wait_ge(root2a_step, 3 * t + 3)
                nc.scalar.activation(hid[:, t % HSLOTS], hid[:, t % HSLOTS], ACT.Identity, bias=sm2[:, t % 2, 2:3],
                                     scale=sm2[:, t % 2, 1:2]).then_inc(norm_done, 1)

            def square(t):
                act.wait_ge(shifted, t + 1)
                if t:
                    act.wait_ge(sq_done, t)
                if t >= 2:
                    act.wait_ge(root2b_step, 3 * (t - 2) + 1)
                nc.scalar.activation(junk[:, :], hid[:, t % HSLOTS], ACT.Square,
                                     accum_out=sm2[:, t % 2, 3:4]).then_inc(sq_done, 1)

            def scale2(t):
                act.wait_ge(sc2_step, 2 * t + 2)
                act.wait_ge(amax2_done, t + 1)
                nc.scalar.activation(hid[:, t % HSLOTS], hid[:, t % HSLOTS], ACT.Identity, bias=ROUND,
                                     scale=sm2[:, t % 2, 8:9]).then_inc(w_done, 1)

            def copy_q2(t):
                act.wait_ge(q2_turned, t + 1)
                if t >= 2:
                    act.wait_ge(mm2_done, t - 1)
                nc.scalar.activation(q2T[:, t % 2].rearrange("p k n -> p (k n)"), tq, ACT.Copy).then_inc(q2T_done, 1)

            def sum_weights(i):
                act.wait_ge((in_w1, in_w2)[i], 16)
                nc.scalar.activation((w1q, w2q)[i][:, :, :].rearrange("p k n -> p (k n)"), w_raw[:, i],
                                     ACT.Abs, accum_out=wabs[:, i:i + 1]).then_inc(wabs_done, 1)

            def silu_z(b):
                act.wait_ge(z_small, 4)
                for h in range(HALVES):
                    j = h * NB + b
                    nc.scalar.activation(siluz[:, h, b, :], x_nat[:, h, b, :], ACT.Silu,
                                         bias=zr[:, 3, j:j + 1], scale=zr[:, 1, j:j + 1]).then_inc(z_ready, 1)

            work = {"silu_u": silu_u, "silu_z": silu_z, "sum_weights": sum_weights, "copy_xd": copy_xd, "dt_bias": dt_bias, "dt_exp": dt_exp,
                    "scale_weights": scale_weights, "copy_q1": copy_q1, "silu": silu, "gelu": gelu, "norm": norm,
                    "square": square, "scale2": scale2, "copy_q2": copy_q2}

            silu_u(0)
            copy_xd(0)
            nc.scalar.preload_act_table_set("natural_log_exp_and_others")
            act.wait_ge(in_chan, 16)
            nc.scalar.activation(negA[:, :, :], chan_sb[:, :, C_A:CH], ACT.Exp).then_inc(expA_done, 1)
            dt_bias(0)
            dt_exp(0)
            for k in range(AHEAD):
                exps(k)
            with_exp = True
            for k in range(END):
                works = [(exps, k + AHEAD)] if k + AHEAD < UNITS else []
                for step, i in works + [(work[name], i) for name, i in act_at.get(k, [])]:
                    if step in (silu_u, silu_z, silu, gelu):
                        with_exp = False
                    elif step in (exps, dt_exp) and not with_exp:
                        nc.scalar.preload_act_table_set("natural_log_exp_and_others")
                        with_exp = True
                    step(i)

        @block.gpsimd
        def _(pool):
            ts, tt = nc.gpsimd.tensor_scalar, nc.gpsimd.tensor_tensor
            nc.gpsimd.memset(ones[:, :], 1.0)
            nc.gpsimd.memset(dA[:, :, :].rearrange("p r (s l) -> p (r s) l", l=L)[:, :, 0:1], 0.0).then_inc(zeros_set, 1)
            nc.gpsimd.memset(m_half[:, :], -0.5).then_inc(consts_set, 1)
            pool.wait_ge(expA_done, 1)
            ts(negA[:, :, :], negA[:, :, :], -1.0, None, ALU.mult).then_inc(negA_ready, 1)

            def z_root():
                pool.wait_ge(z_aggr, HALVES * NB)
                pool.wait_ge(consts_set, 1)
                ts(zr[:, 0, :], zmv[:, :, 1], EPS, None, ALU.add).then_inc(z_small, 1)
                pool.wait_ge(z_small, 1)
                tt(zr[:, 1, :], zr[:, 0, :], m_half[:, :], ALU.pow).then_inc(z_small, 1)
                pool.wait_ge(z_small, 2)
                tt(zr[:, 2, :], zr[:, 1, :], zmv[:, :, 0], ALU.mult).then_inc(z_small, 1)
                pool.wait_ge(z_small, 3)
                ts(zr[:, 3, :], zr[:, 2, :], -1.0, None, ALU.mult).then_inc(z_small, 1)

            def dt_series(b):
                n = parts_before(b)
                pool.wait_ge(dt_e, n + 1)
                pool.wait_ge(dt_step, 3 * n)
                ts(sp_ser[:, :, :], sp_e[:, :, :], -0.5, 1.0, ALU.mult, ALU.add).then_inc(dt_ser, 1)
                pool.wait_ge(dt_ser, 2 * n + 1)
                tt(sp_ser[:, :, :], sp_ser[:, :, :], sp_e[:, :, :], ALU.mult).then_inc(dt_ser, 1)

            def prod(k):
                b, h, ng = where(k)
                pool.wait_ge(c_in[ng], 16 * (b + 1))
                pool.wait_ge(scanned, k + 1)
                s = st[:, k % ST_RING, :]
                tt(s, s, bc[:, ng, 1].rearrange("p s l -> p (s l)"), ALU.mult).then_inc(prod_done, 1)

            def root1(b):
                pool.wait_ge(mv1_done, TPB * (b + 1))
                if b:
                    pool.wait_ge(sc1_step, 5 * b)
                ts(sm1[:, 0, :], mv1[:, :, 1], 1.0 + EPS, EPS * EPS, ALU.mult, ALU.add).then_inc(root1_step, 1)
                pool.wait_ge(root1_step, 3 * b + 1)
                tt(sm1[:, 1, :], sm1[:, 0, :], m_half[:, 0:TPB], ALU.pow).then_inc(root1_step, 1)
                pool.wait_ge(root1_step, 3 * b + 2)
                ts(sm1[:, 2, :], sm1[:, 1, :], LEVELS / EPS, None, ALU.mult).then_inc(root1_step, 1)

            def add_b2(b):
                pool.wait_ge(xc_done, TPB * (b + 1))
                if b == 0:
                    pool.wait_ge(in_rows, 16)
                tt(x_nat[:, :, b, :], x_nat[:, :, b, :],
                   rows_sb[:, 3 * HID:3 * HID + D].unsqueeze(1).to_broadcast([P, TPB, D]), ALU.add).then_inc(b2_added, 1)

            def root2a(t):
                s = sm2[:, t % 2, :]
                pool.wait_ge(mv2_done, t + 1)
                if t >= 2:
                    pool.wait_ge(norm_done, t - 1)
                ts(s[:, 0:1], mv2[:, t % 2, 1:2], EPS, None, ALU.add).then_inc(root2a_step, 1)
                pool.wait_ge(root2a_step, 3 * t + 1)
                tt(s[:, 1:2], s[:, 0:1], m_half[:, 0:1], ALU.pow).then_inc(root2a_step, 1)
                pool.wait_ge(root2a_step, 3 * t + 2)
                ts(s[:, 2:3], mv2[:, t % 2, 0:1], s[:, 1:2], -1.0, ALU.mult, ALU.mult).then_inc(root2a_step, 1)

            def shift(t):
                if t >= TILES - TPB:
                    return
                h = hid[:, t % HSLOTS]
                pool.wait_ge(gained, t + 1)
                tt(h, h, rows_sb[:, 2 * HID:3 * HID], ALU.add).then_inc(shifted, 1)

            def root2b(t):
                s = sm2[:, t % 2, :]
                pool.wait_ge(sq_done, t + 1)
                if t >= 2:
                    pool.wait_ge(sc2_step, 2 * (t - 1))
                    pool.wait_ge(out_scaled, 2 * (t - 1))
                ts(s[:, 4:5], s[:, 3:4], 1.0 / HID, EPS, ALU.mult, ALU.add).then_inc(root2b_step, 1)
                pool.wait_ge(root2b_step, 3 * t + 1)
                tt(s[:, 5:6], s[:, 4:5], m_half[:, 0:1], ALU.pow).then_inc(root2b_step, 1)
                pool.wait_ge(root2b_step, 3 * t + 2)
                ts(s[:, 6:7], s[:, 5:6], LEVELS / EPS, None, ALU.mult).then_inc(root2b_step, 1)

            def out_scale(t):
                s = sm2[:, t % 2, :]
                pool.wait_ge(root2b_step, 3 * t + 2)
                pool.wait_ge(amax2_done, t + 1)
                pool.wait_ge(wmean_step, 4)
                if t >= 2:
                    pool.wait_ge(res_done, t - 1)
                ts(s[:, 9:10], am2[:, t % 2:t % 2 + 1], s[:, 5:6], EPS, ALU.mult, ALU.max).then_inc(out_scaled, 1)
                pool.wait_ge(out_scaled, 2 * t + 1)
                ts(s[:, 10:11], s[:, 9:10], wmean[:, 1, 2:3], None, ALU.mult).then_inc(out_scaled, 1)

            def quant2(t):
                pool.wait_ge(w_done, t + 1)
                if t >= 2:
                    pool.wait_ge(q2_turned, t - 1)
                ts(q2[:, t % 2, :], hid[:, t % HSLOTS], 1.0, -ROUND, ALU.mult, ALU.add).then_inc(q2_done, 1)

            work = {"dt_series": dt_series, "root1": root1, "add_b2": add_b2, "root2a": root2a, "shift": shift,
                    "root2b": root2b, "out_scale": out_scale, "quant2": quant2}
            z_root()
            for k in range(END):
                if k < UNITS:
                    prod(k)
                for name, i in pool_at.get(k, []):
                    work[name](i)

        @block.vector
        def _(dve):
            ts, tt, stt = nc.vector.tensor_scalar, nc.vector.tensor_tensor, nc.vector.scalar_tensor_tensor

            def conv():
                dve.wait_ge(xin_ready, 1)
                for s in range(TAPS):
                    for h in range(HALVES):
                        w = chan_sb[:, h, C_CONV + TAPS - 1 - s:C_CONV + TAPS - s]
                        x_in, o = xin[0][:, h * L:(h + 1) * L - s], cv[:, h, 0, s:L]
                        if s == 0:
                            ins = ts(o, x_in, w, chan_sb[:, h, C_CB:C_CB + 1], ALU.mult, ALU.add)
                        else:
                            dve.wait_ge(conv_step, 2 * (s - 1) + h + 1)
                            ins = stt(out=o, in0=x_in, scalar=w, in1=o, op0=ALU.mult, op1=ALU.add)
                        ins.then_inc(conv_step, 1)

            def dt_neg(b):
                for n, hs in parts(b):
                    dve.wait_ge(dt_v, HALVES * b + hs.stop)
                    if b:
                        dve.wait_ge(dt_step, 3 * n)
                    stt(out=sp_e[:, hs, :], in0=sp_v[:, hs, :], scalar=-1.0, in1=sp_v[:, hs, :], op0=ALU.mult,
                        op1=ALU.min).then_inc(dt_negd, 1)

            def mask_part(n, hs):
                dve.wait_ge(dt_e, n + 1)
                ts(sp_mask[:, hs, :], sp_e[:, hs, :], SMALL_E, None, ALU.is_lt).then_inc(dt_step, 1)
                if n < HALVES:
                    ts(sp_ser[:, hs, :], sp_e[:, hs, :], -0.5, 1.0, ALU.mult, ALU.add).then_inc(dt_ser, 1)
                    dve.wait_ge(dt_ser, 2 * n + 1)
                    tt(sp_ser[:, hs, :], sp_ser[:, hs, :], sp_e[:, hs, :], ALU.mult).then_inc(dt_ser, 1)

            def sum_part(b, n, hs):
                dve.wait_ge(dt_step, 3 * n + 1)
                dve.wait_ge(dt_ln, n + 1)
                dve.wait_ge(dt_ser, 2 * n + 2)
                flat = "p h l -> p (h l)"
                nc.vector.copy_predicated(sp_ln[:, hs, :].rearrange(flat), sp_mask[:, hs, :].rearrange(flat).bitcast(I32),
                                          sp_ser[:, hs, :].rearrange(flat)).then_inc(dt_cp, 1)
                dve.wait_ge(dt_cp, n + 1)
                if b >= 2:
                    dve.wait_ge(exp_done, UPB * (b - 1))
                    dve.wait_ge(dbu_done, UPB * (b - 1))
                stt(out=dt[:, hs, b % 2, :], in0=sp_v[:, hs, :], scalar=0.0, in1=sp_ln[:, hs, :], op0=ALU.max,
                    op1=ALU.add).then_inc(dt_step, 1)
                dve.wait_ge(dt_step, 3 * n + 2)
                tt(dtu[:, hs, b % 2, :], dt[:, hs, b % 2, :], u[:, hs, b, :], ALU.mult).then_inc(dt_step, 1)

            def dt_mask(b):
                mask_part(*parts(b)[0])

            def dt_sum(b):
                sum_part(b, *parts(b)[0])

            def dt_half(h):
                mask_part(*parts(0)[h])
                sum_part(0, *parts(0)[h])

            def mult(k):
                b, h, ng = where(k)
                dve.wait_ge(b_in[ng], 16 * (b + 1))
                if ng == 0:
                    dve.wait_ge(dt_step, 3 * (parts_before(b) if b else h) + 3)
                if k >= DBU_RING:
                    dve.wait_ge(scanned, k - DBU_RING + 1)
                tt(dBu[:, k % DBU_RING, :].rearrange("p (s l) -> p s l", s=SG),
                   dtu[:, h, b % 2, :].unsqueeze(1).to_broadcast([P, SG, L]), bc[:, ng, 0], ALU.mult).then_inc(dbu_done, 1)

            def scan(k):
                dve.wait_ge(dbu_done, k + 1)
                dve.wait_ge(exp_done, k + 1)
                if k >= ST_RING:
                    dve.wait_ge(summed, k - ST_RING + 1)
                nc.vector.tensor_tensor_scan(st[:, k % ST_RING, :], dA[:, k % DA_RING, :], dBu[:, k % DBU_RING, :], 0.0,
                                             ALU.mult, ALU.add).then_inc(scanned, 1)

            def clip_weights(i):
                n = 2 * i
                q = (w1q if i == 0 else w2q)[:, :, :].rearrange("p k n -> p (k n)")
                dve.wait_ge(w_scaled, i + 1)
                ts(w_raw[:, i], w_raw[:, i], ROUND, -1.0, ALU.subtract, ALU.max).then_inc(w_clip, 1)
                dve.wait_ge(w_clip, n + 1)
                ts(q, w_raw[:, i], 1.0, None, ALU.min).then_inc(w_clip, 1)

            def gate(g):
                b, h = g // 2, g % 2
                dve.wait_ge(summed, GROUPS * (g + 1))
                dve.wait_ge(z_ready, HALVES * (b + 1))
                if g >= 2:
                    dve.wait_ge(y_turned, g - 1)
                tt(yg[:, g % 2, :], yacc, siluz[:, h, b, :], ALU.mult).then_inc(gate_step, 1)

            def add_x1(g):
                b, h = g // 2, g % 2
                dve.wait_ge(y_turned, g + 1)
                tt(x_nat[:, :, b, h * P:(h + 1) * P], x_nat[:, :, b, h * P:(h + 1) * P],
                   yT.rearrange("p (t d) -> p t d", t=TPB), ALU.add).then_inc(x1_half, 1)

            def ln1(b):
                dve.wait_ge(x1_half, 2 * b + 2)
                for i in range(TPB):
                    nc.vector.bn_stats(stats[:, 8 + i, :], x_nat[:, i, b, :]).then_inc(bn1_done, 1)
                if b:
                    dve.wait_ge(root1_step, 3 * b)
                for i in range(TPB):
                    dve.wait_ge(bn1_done, TPB * b + i + 1)
                    nc.vector.bn_aggr(mv1[:, i, :], stats[:, 8 + i, :]).then_inc(mv1_done, 1)
                for i in range(TPB):
                    dve.wait_ge(mv1_done, TPB * b + i + 1)
                    ts(xc[:, i, :], x_nat[:, i, b, :], mv1[:, i, 0:1], None, ALU.subtract).then_inc(xc_done, 1)
                dve.wait_ge(xc_done, TPB * (b + 1))
                nc.vector.tensor_reduce(amax1[:, :], xc[:, :, :], AX.X, ALU.max, apply_absolute_value=True)\
                    .then_inc(amax1_done, 1)

            def quant1(b):
                n, s = 5 * b, [sm1[:, j, :] for j in range(8)]
                dve.wait_ge(amax1_done, b + 1)
                if b:
                    dve.wait_ge(silu_done, TPB * b)
                nc.vector.reciprocal(s[5], amax1[:, :]).then_inc(sc1_step, 1)
                dve.wait_ge(root1_step, 3 * b + 3)
                tt(s[3], amax1[:, :], s[1], ALU.mult).then_inc(sc1_step, 1)
                dve.wait_ge(sc1_step, n + 1)
                stt(out=s[6], in0=s[5], scalar=LEVELS, in1=s[2], op0=ALU.mult, op1=ALU.min).then_inc(sc1_step, 1)
                dve.wait_ge(wmean_step, 4)
                dve.wait_ge(sc1_step, n + 2)
                ts(s[4], s[3], EPS, wmean[:, 0, 2:3], ALU.max, ALU.mult).then_inc(sc1_step, 1)
                dve.wait_ge(sc1_step, n + 3)
                for i in range(TPB):
                    ts(xc[:, i, :], xc[:, i, :], s[6][:, i:i + 1], ROUND, ALU.mult, ALU.add).then_inc(q1_scaled, 1)
                dve.wait_ge(sc1_step, n + 4)
                nc.vector.reciprocal(s[7], s[4]).then_inc(sc1_step, 1)
                dve.wait_ge(q1_scaled, TPB * (b + 1))
                if b:
                    dve.wait_ge(q1_turned, b)
                ts(q1[:, :, :], xc[:, :, :], ROUND, None, ALU.subtract).then_inc(q1_done, 1)
                dve.wait_ge(sc1_step, n + 5)
                if b:
                    dve.wait_ge(mm1_done, TPB * b)
                for i in range(TPB):
                    ts(diag[:, i, :], id_f[:, :], s[7][:, i:i + 1], None, ALU.mult).then_inc(diag_done, 1)

            def bn2(t):
                dve.wait_ge(gelu_done, t + 1)
                o = 10 + 2 * (t % 2)
                for i in range(2):
                    nc.vector.bn_stats(stats[:, o + i, :], hid[:, t % HSLOTS, 512 * i:512 * (i + 1)]).then_inc(bn2_done, 1)
                dve.wait_ge(bn2_done, 2 * t + 2)
                if t >= 2:
                    dve.wait_ge(root2a_step, 3 * (t - 1))
                nc.vector.bn_aggr(mv2[:, t % 2, :], stats[:, o:o + 2, :].rearrange("p a b -> p (a b)")).then_inc(mv2_done, 1)

            def gain(t):
                h = hid[:, t % HSLOTS]
                if t >= TILES - TPB:
                    dve.wait_ge(mv2_done, t + 1)
                    stt(out=h, in0=h, scalar=mv2[:, t % 2, 0:1], in1=rows_sb[:, HID:2 * HID], op0=ALU.subtract,
                        op1=ALU.mult).then_inc(gained, 1)
                    dve.wait_ge(root2a_step, 3 * t + 2)
                    dve.wait_ge(gained, t + 1)
                    stt(out=h, in0=h, scalar=sm2[:, t % 2, 1:2], in1=rows_sb[:, 2 * HID:3 * HID], op0=ALU.mult,
                        op1=ALU.add).then_inc(shifted, 1)
                    return
                dve.wait_ge(norm_done, t + 1)
                tt(h, h, rows_sb[:, HID:2 * HID], ALU.mult).then_inc(gained, 1)

            def do_amax2(t):
                dve.wait_ge(shifted, t + 1)
                if t >= 2:
                    dve.wait_ge(sc2_step, 2 * (t - 1))
                    dve.wait_ge(out_scaled, 2 * (t - 1))
                nc.vector.tensor_reduce(am2[:, t % 2:t % 2 + 1], hid[:, t % HSLOTS], AX.X, ALU.max,
                                        apply_absolute_value=True).then_inc(amax2_done, 1)

            def scales2(t):
                s = [sm2[:, t % 2, j:j + 1] for j in range(12)]
                dve.wait_ge(amax2_done, t + 1)
                if t >= 2:
                    dve.wait_ge(w_done, t - 1)
                nc.vector.reciprocal(s[7], am2[:, t % 2:t % 2 + 1]).then_inc(sc2_step, 1)
                dve.wait_ge(sc2_step, 2 * t + 1)
                dve.wait_ge(root2b_step, 3 * t + 3)
                ts(s[8], s[7], LEVELS, s[6], ALU.mult, ALU.min).then_inc(sc2_step, 1)

            def quant2(t):
                dve.wait_ge(w_done, t + 1)
                dve.wait_ge(q2_turned, t - 1)
                ts(q2[:, t % 2, :], hid[:, t % HSLOTS], ROUND, None, ALU.subtract).then_inc(q2_done, 1)

            def result(t):
                b, i = t // TPB, t % TPB
                dve.wait_ge(mm2_done, t + 1)
                dve.wait_ge(out_scaled, 2 * t + 2)
                dve.wait_ge(b2_added, b + 1)
                if t >= 2:
                    dve.wait_ge(out_done[t % 2], 16 * (t // 2))
                stt(out=res[:, t % 2, :], in0=mm2, scalar=sm2[:, t % 2, 10:11], in1=x_nat[:, i, b, :],
                    op0=ALU.mult, op1=ALU.add).then_inc(res_done, 1)

            def z_norm():
                dve.wait_ge(in_x, 16 * HALVES)
                for j in range(HALVES * NB):
                    nc.vector.bn_stats(stats[:, j, :], x_nat[:, j // NB, j % NB, :]).then_inc(z_stats, 1)
                for j in range(HALVES * NB):
                    dve.wait_ge(z_stats, j + 1)
                    nc.vector.bn_aggr(zmv[:, j, :], stats[:, j, :]).then_inc(z_aggr, 1)

            def mean_weights(_):
                dve.wait_ge(wsum_ready, 1)
                for i in range(2):
                    ts(wmean[:, i, 0:1], bank(6)[:, i:i + 1], 1.0 / (HID * D), EPS, ALU.mult, ALU.max)\
                        .then_inc(wmean_step, 1)
                dve.wait_ge(wmean_step, 2)
                nc.vector.reciprocal(wmean[:, :, 1], wmean[:, :, 0]).then_inc(wmean_step, 1)
                ts(wmean[:, :, 2], wmean[:, :, 0], 1.0 / LEVELS, None, ALU.mult).then_inc(wmean_step, 1)

            dve.wait_ge(in_chan, 16)
            conv()
            dve.wait_ge(in_taps, 16)
            dve.wait_ge(in_inw, 16)
            tt(inw_taps[:, :, :], taps_sb[:, :, :], inw_sb[:, :].unsqueeze(1).to_broadcast([P, TAPS, D]), ALU.mult)\
                .then_inc(taps_scaled, 1)
            z_norm()
            dt_neg(0)
            dve.wait_ge(in_id, 16)
            nc.vector.tensor_copy(id_b[:, :], id_f[:, :]).then_inc(id_cast, 1)
            for h in range(HALVES):
                ts(diag_D[:, h, :], id_f[:, :], chan_sb[:, h, C_D:C_D + 1], None, ALU.mult).then_inc(diag_D_done, 1)
            dt_half(0)
            mult(0)
            work = {"wmean": mean_weights, "dt_half": dt_half, "dt_neg": dt_neg, "dt_mask": dt_mask, "dt_sum": dt_sum, "clip_weights": clip_weights,
                    "gate": gate, "x1": add_x1, "ln1": ln1, "quant1": quant1, "bn2": bn2, "gain": gain,
                    "amax2": do_amax2, "scales2": scales2, "quant2": quant2, "res": result}
            for k in range(END):
                if k + 1 < UNITS:
                    mult(k + 1)
                if k < UNITS:
                    scan(k)
                for name, i in vec_at.get(k, []):
                    work[name](i)


def kernel(x, ctx_1024, L0_xattn_in_proj_w, L0_xattn_conv_w, L0_xattn_conv_b, L0_xattn_x_proj_w,
           L0_xattn_dt_proj_w, L0_xattn_dt_proj_b, L0_xattn_A_log, L0_xattn_D, L0_ffn_w1, L0_ffn_b1,
           L0_ffn_ln_g, L0_ffn_ln_b, L0_ffn_w2, L0_ffn_b2):
    import numpy as np
    import concourse.bacc as bacc
    from concourse.bass_utils import run_bass_kernel_spmd

    def halves(a):
        return np.ascontiguousarray(a.reshape(HALVES, P, -1).transpose(1, 0, 2))

    f = np.asarray
    xp = f(L0_xattn_x_proj_w)
    bcw = xp[R:].reshape(2, GROUPS, SG, D).transpose(1, 0, 2, 3).reshape(2 * NS, D)
    chan = np.concatenate([f(L0_xattn_conv_w)[:, 0, :], f(L0_xattn_conv_b)[:, None], f(L0_xattn_dt_proj_b)[:, None],
                           f(L0_xattn_D)[:, None], f(L0_xattn_A_log)], axis=1)
    data = {
        "x": np.ascontiguousarray(f(x)),
        "ctxT": np.ascontiguousarray(f(ctx_1024).reshape(NB * L, DM).T),
        "inwT": np.ascontiguousarray(f(L0_xattn_in_proj_w).T),
        "xprojT": halves(np.concatenate([bcw, xp[:R]], axis=0).T),
        "dtpT": np.ascontiguousarray(f(L0_xattn_dt_proj_w).T),
        "chan": halves(chan),
        "taps": np.ascontiguousarray(f(L0_xattn_conv_w)[:, 0, ::-1].T).reshape(TAPS * D),
        "w1T": np.ascontiguousarray(f(L0_ffn_w1).T),
        "w2T": np.ascontiguousarray(f(L0_ffn_w2).T),
        "rows": np.concatenate([f(L0_ffn_b1), f(L0_ffn_ln_g), f(L0_ffn_ln_b), f(L0_ffn_b2)]),
        "ident": np.eye(P, dtype=np.float32),
    }
    nc = bacc.Bacc("TRN2", target_bir_lowering=False, num_devices=1)
    args = [nc.dram_tensor(n, a.shape, mybir.dt.from_np(a.dtype), kind="ExternalInput").ap() for n, a in data.items()]
    spread = nc.dram_tensor("spread", (NB, 2 * NS, L), F32, kind="Internal").ap()
    out = nc.dram_tensor("out", (NB, L, D), F32, kind="ExternalOutput").ap()
    mixer_ffn(nc, *args, spread, out)
    r = run_bass_kernel_spmd(nc, [data], core_ids=[0])
    return r.results[0]["out"]
```
